# Optimizing a Trainium2 kernel written in Bass

```python
import numpy as np
import jax
import jax.numpy as jnp

def _softmax(x, axis=-1):
    return jax.nn.softmax(x, axis=axis)

def _gelu(x):
    return jax.nn.gelu(x, approximate=True)

def _silu(x):
    return jax.nn.silu(x)

def _sigmoid(x):
    return jax.nn.sigmoid(x)

def _layernorm(x, axis=-1, eps=1e-05):
    m = jnp.mean(x, axis=axis, keepdims=True)
    v = jnp.var(x, axis=axis, keepdims=True)
    return (x - m) / jnp.sqrt(v + eps)

def _scatter_add(tgt, idx, src, axis=0):
    return tgt.at[idx].add(src)

def _segment_sum(src, seg, n):
    return jax.ops.segment_sum(src, seg, n)
kernel_name = 'mk_hybrid_d1_jaxref_r8_825406'

def setup_inputs(seed: int=0):
    np.random.seed(seed)
    _w = jnp.asarray

    def _L0_attn_a_setup():
        import jax, jax.numpy as jnp
        import numpy as np
        NEG = -1000000000.0

        def _attention(x, Wq, bq, Wk, bk, Wv, bv, Wo, num_heads=16):
            B, N, E = x.shape
            H = num_heads
            D = E // H
            scale = D ** (-0.5)
            q = (jnp.einsum('bne,fe->bnf', x, Wq) + bq).reshape(B, N, H, D).transpose(0, 2, 1, 3)
            k = (jnp.einsum('bne,fe->bnf', x, Wk) + bk).reshape(B, N, H, D).transpose(0, 2, 1, 3)
            v = (jnp.einsum('bne,fe->bnf', x, Wv) + bv).reshape(B, N, H, D).transpose(0, 2, 1, 3)
            scores = jnp.einsum('bhqd,bhkd->bhqk', q, k) * scale
            scores = scores.at[:, :, 0, -1].set(NEG)
            scores = scores.at[:, :, -1, 0].set(NEG)
            weights = jax.nn.softmax(scores, axis=-1)
            out = jnp.einsum('bhqk,bhkd->bhqd', weights, v)
            out = out.transpose(0, 2, 1, 3).reshape(B, N, E)
            return jnp.einsum('bne,fe->bnf', out, Wo)
        key = jax.random.key(seed)
        ks = jax.random.split(key, 8)
        B, N, E = (4, 256, 128)
        s = E ** (-0.5)
        return {'x': jax.random.normal(ks[0], (B, N, E), jnp.float32), 'Wq': jax.random.normal(ks[1], (E, E), jnp.float32) * s, 'bq': jax.random.normal(ks[2], (E,), jnp.float32) * 0.02, 'Wk': jax.random.normal(ks[3], (E, E), jnp.float32) * s, 'bk': jax.random.normal(ks[4], (E,), jnp.float32) * 0.02, 'Wv': jax.random.normal(ks[5], (E, E), jnp.float32) * s, 'bv': jax.random.normal(ks[6], (E,), jnp.float32) * 0.02, 'Wo': jax.random.normal(ks[7], (E, E), jnp.float32) * s}
    _L0_attn_a_in = _L0_attn_a_setup()

    def _L0_attn_b_setup():
        import jax, jax.numpy as jnp
        import numpy as np
        N_FILTERS = 128
        N_HEADS = 16
        key = jax.random.key(seed)
        k1, k2, k3 = jax.random.split(key, 3)
        x = jax.random.normal(k1, (8, 128, N_FILTERS), dtype=jnp.float32)
        w_qkv = jax.random.normal(k2, (N_FILTERS, N_FILTERS * 3), dtype=jnp.float32) * (0.02 / N_FILTERS) ** 0.5
        w_out = jax.random.normal(k3, (N_FILTERS, N_FILTERS), dtype=jnp.float32) * (0.02 / N_FILTERS) ** 0.5
        return {'x': x, 'w_qkv': w_qkv, 'w_out': w_out}
    _L0_attn_b_in = _L0_attn_b_setup()

    def _L0_ffn_setup():
        import jax, jax.numpy as jnp
        import numpy as np
        TOP_K = 2
        key = jax.random.key(seed)
        ks = jax.random.split(key, 6)
        B, S, D, BN, E = (32, 256, 128, 64, 8)
        return {'x': jax.random.normal(ks[0], (B, S, D), dtype=jnp.float32), 'gate_w': jax.random.normal(ks[1], (E, D), dtype=jnp.float32) * 0.02, 'down_w': jax.random.normal(ks[2], (E, BN, D), dtype=jnp.float32) * 0.02, 'down_b': jax.random.normal(ks[3], (E, BN), dtype=jnp.float32) * 0.02, 'up_w': jax.random.normal(ks[4], (E, D, BN), dtype=jnp.float32) * 0.02, 'up_b': jax.random.normal(ks[5], (E, D), dtype=jnp.float32) * 0.02}
    _L0_ffn_in = _L0_ffn_setup()
    _d = {'L0_attn_a_x': _L0_attn_a_in['x'], 'L0_attn_a_Wq': _L0_attn_a_in['Wq'], 'L0_attn_a_bq': _L0_attn_a_in['bq'], 'L0_attn_a_Wk': _L0_attn_a_in['Wk'], 'L0_attn_a_bk': _L0_attn_a_in['bk'], 'L0_attn_a_Wv': _L0_attn_a_in['Wv'], 'L0_attn_a_bv': _L0_attn_a_in['bv'], 'L0_attn_a_Wo': _L0_attn_a_in['Wo'], 'L0_attn_b_w_qkv': _L0_attn_b_in['w_qkv'], 'L0_attn_b_w_out': _L0_attn_b_in['w_out'], 'L0_ffn_gate_w': _L0_ffn_in['gate_w'], 'L0_ffn_down_w': _L0_ffn_in['down_w'], 'L0_ffn_down_b': _L0_ffn_in['down_b'], 'L0_ffn_up_w': _L0_ffn_in['up_w'], 'L0_ffn_up_b': _L0_ffn_in['up_b']}
    _x0 = _d['L0_attn_a_x']
    _d['L0_attn_a_x'] = jax.random.normal(jax.random.fold_in(jax.random.key(seed), 1), (32, 256, 128), dtype=_x0.dtype)
    del _x0
    return _d

def reference(L0_attn_a_x, L0_attn_a_Wq, L0_attn_a_bq, L0_attn_a_Wk, L0_attn_a_bk, L0_attn_a_Wv, L0_attn_a_bv, L0_attn_a_Wo, L0_attn_b_w_qkv, L0_attn_b_w_out, L0_ffn_gate_w, L0_ffn_down_w, L0_ffn_down_b, L0_ffn_up_w, L0_ffn_up_b):

    def _L0_attn_a_ref(x, Wq, bq, Wk, bk, Wv, bv, Wo):
        import jax, jax.numpy as jnp
        import numpy as np
        NEG = -1000000000.0

        def _attention(x, Wq, bq, Wk, bk, Wv, bv, Wo, num_heads=16):
            B, N, E = x.shape
            H = num_heads
            D = E // H
            scale = D ** (-0.5)
            q = (jnp.einsum('bne,fe->bnf', x, Wq) + bq).reshape(B, N, H, D).transpose(0, 2, 1, 3)
            k = (jnp.einsum('bne,fe->bnf', x, Wk) + bk).reshape(B, N, H, D).transpose(0, 2, 1, 3)
            v = (jnp.einsum('bne,fe->bnf', x, Wv) + bv).reshape(B, N, H, D).transpose(0, 2, 1, 3)
            scores = jnp.einsum('bhqd,bhkd->bhqk', q, k) * scale
            scores = scores.at[:, :, 0, -1].set(NEG)
            scores = scores.at[:, :, -1, 0].set(NEG)
            weights = jax.nn.softmax(scores, axis=-1)
            out = jnp.einsum('bhqk,bhkd->bhqd', weights, v)
            out = out.transpose(0, 2, 1, 3).reshape(B, N, E)
            return jnp.einsum('bne,fe->bnf', out, Wo)
        return _attention(x, Wq, bq, Wk, bk, Wv, bv, Wo, num_heads=16)

    def _L0_attn_b_ref(x, w_qkv, w_out):
        import jax, jax.numpy as jnp
        import numpy as np
        N_FILTERS = 128
        N_HEADS = 16
        b, n, c = x.shape
        h = N_HEADS
        d = c // h
        qkv = jnp.einsum('bnc,ce->bne', x, w_qkv)
        q, k, v = jnp.split(qkv, 3, axis=-1)
        to_heads = lambda t: t.reshape(b, n, h, d).transpose(0, 2, 1, 3)
        q, k, v = (to_heads(q), to_heads(k), to_heads(v))
        scale = jnp.sqrt(jnp.asarray(c, jnp.float32))
        attn = jnp.einsum('bhnd,bhmd->bhnm', q, k) / scale
        attn = jax.nn.softmax(attn, axis=-1)
        out = jnp.einsum('bhnm,bhmd->bhnd', attn, v)
        out = out.transpose(0, 2, 1, 3).reshape(b, n, c)
        return jnp.einsum('bnc,co->bno', out, w_out)

    def _L0_ffn_ref(x, gate_w, down_w, down_b, up_w, up_b):
        import jax, jax.numpy as jnp
        import numpy as np
        TOP_K = 2
        pooled = x.mean(axis=1)
        gate = jax.nn.softmax(pooled @ gate_w.T, axis=-1)
        top_w, top_i = jax.lax.top_k(gate, TOP_K)
        top_w = top_w / (top_w.sum(axis=-1, keepdims=True) + 1e-08)
        Wd = down_w[top_i]
        bd = down_b[top_i]
        Wu = up_w[top_i]
        bu = up_b[top_i]
        h = jax.nn.gelu(jnp.einsum('bsd,bkcd->bksc', x, Wd) + bd[:, :, None, :], approximate=False)
        h = h * top_w[:, :, None, None]
        out = jnp.einsum('bksc,bkdc->bsd', h, Wu)
        out = out + (top_w[:, :, None] * bu).sum(axis=1)[:, None, :]
        return out
    x = L0_attn_a_x
    x = x + _L0_attn_a_ref(_layernorm(x, axis=-1), L0_attn_a_Wq, L0_attn_a_bq, L0_attn_a_Wk, L0_attn_a_bk, L0_attn_a_Wv, L0_attn_a_bv, L0_attn_a_Wo)
    x = x + _L0_ffn_ref(_layernorm(x, axis=-1), L0_ffn_gate_w, L0_ffn_down_w, L0_ffn_down_b, L0_ffn_up_w, L0_ffn_up_b)
    x = x + _L0_attn_b_ref(_layernorm(x, axis=-1), L0_attn_b_w_qkv, L0_attn_b_w_out)
    x = x + _L0_ffn_ref(_layernorm(x, axis=-1), L0_ffn_gate_w, L0_ffn_down_w, L0_ffn_down_b, L0_ffn_up_w, L0_ffn_up_b)
    return x

_drawn_inputs = setup_inputs


def setup_inputs(seed=0):
    import zlib

    import numpy as np

    out = dict(_drawn_inputs(seed))
    spreads = {}
    factors = {'L0_attn_a_bq': 8.0,
     'L0_attn_a_bk': 64.0,
     'L0_attn_b_w_qkv': 8.0,
     'L0_attn_b_w_out': 8.0,
     'L0_ffn_down_b': 23.333}
    for name, (base, spread) in spreads.items():
        noise = np.random.default_rng([zlib.crc32(name.encode()), seed]).standard_normal(out[name].shape)
        drawn = base * np.exp(spread * noise) if base else spread * noise
        out[name] = jnp.asarray(drawn.astype(out[name].dtype))
    for name, factor in factors.items():
        out[name] = (out[name] * factor).astype(out[name].dtype)
    return out
```

```python
import numpy as np

import concourse.bass as bass
from concourse import mybir
from contextlib import ExitStack

FP32 = mybir.dt.float32
BF16 = mybir.dt.bfloat16
U32 = mybir.dt.uint32
ALU = mybir.AluOpType
ACT = mybir.ActivationFunctionType
AX = mybir.AxisListType

P = 128
ITEMS, TOKENS, WIDTH = 32, 256, 128
TILES = TOKENS // P
HEADS, HEAD = 16, 8
PAIRS = HEADS // 2
EXPERTS, HIDDEN, TOP = 8, 64, 2
EPS = 1e-5
NEG = -1.0e30

Q_PARTS = (0, 0, 0, 1, 1, 2)
K_PARTS = (0, 1, 2, 0, 1, 0)
SLOTS = len(Q_PARTS)
BLOCK = 64
MASK_ROW = SLOTS * HEAD
MAX_ROW = MASK_ROW + 2
ALL_SLOTS = BLOCK // HEAD

RING = 4
GROUPS, PER_GROUP = 4, 4


def rows_of_constants():
    tail = np.zeros((2, BLOCK - MASK_ROW, 2, TOKENS), np.float32)
    tail[0, 0, 0, 0] = NEG
    tail[0, 1, 0, TOKENS - 1] = NEG
    tail[:, 0, 1, TOKENS - 1] = 1.0
    tail[:, 1, 1, 0] = 1.0
    tail[:, 2:5, 1, :] = 1.0
    return tail


def build(nc, x_in, attn_w, attn_b, gate_w, down_w, down_b, up_w, up_b, tail_c, ident_c, iota_c, out):
    ctx = ExitStack()
    with ctx:
        def sb(name, shape, dt=FP32):
            return ctx.enter_context(nc.sbuf_tensor(name, shape, dt))

        def sem(name):
            return ctx.enter_context(nc.semaphore(name))

        x = sb("x", [P, ITEMS * TILES, WIDTH])
        normT = sb("normT", [P, ITEMS, TOKENS])
        pooled = sb("pooled", [P, ITEMS])
        q_stack = [sb(f"q_stack{r}", [P, PAIRS, TOKENS], BF16) for r in range(RING)]
        k_stack = [sb(f"k_stack{r}", [P, PAIRS, 2, TOKENS], BF16) for r in range(RING)]
        values = [sb(f"values{r}", [P, TILES, HEADS, 32]) for r in range(RING)]
        qk32 = [sb(f"qk32_{i}", [P, 2, TOKENS]) for i in range(2)]
        rest = [sb(f"rest{i}", [P, 2, TOKENS]) for i in range(2)]
        parts = [sb(f"parts{i}", [P, 3, 2, TOKENS], BF16) for i in range(2)]
        probs_both = sb("probs", [P, 2, PER_GROUP, TILES, TOKENS])
        probs = [probs_both[:, i] for i in range(2)]
        xn = [sb(f"xn{i}", [P, TILES, WIDTH]) for i in range(2)]
        yn = [sb(f"yn{i}", [P, TILES, WIDTH]) for i in range(2)]
        xnT = [sb(f"xnT{i}", [P, TOKENS]) for i in range(2)]
        raw = [sb(f"raw{i}", [P, TILES, 6]) for i in range(4)]
        mv = [sb(f"mv{i}", [P, TILES, 2]) for i in range(4)]
        varp = [sb(f"varp{i}", [P, TILES]) for i in range(4)]
        rstd = [sb(f"rstd{i}", [P, TILES]) for i in range(4)]
        nmax = [sb(f"nmax{i}", [P, TILES, HEADS]) for i in range(2)]
        mrest = [sb(f"mrest{i}", [P, TILES * HEADS]) for i in range(2)]
        mparts = [sb(f"mparts{i}", [P, TILES * 2, 3, PAIRS], BF16) for i in range(2)]
        maxT = [sb(f"maxT{i}", [2 * 3 * PAIRS, TOKENS], BF16) for i in range(2)]
        oT = [sb(f"oT{i}", [P, GROUPS, TOKENS]) for i in range(2)]
        rsum = sb("rsum", [P, TILES, HEADS])
        o = sb("o", [P, TILES, WIDTH])
        onT = sb("onT", [P, TOKENS])
        wa = sb("wa", [P, 4 * WIDTH + 3])
        wb = sb("wb", [P, 4 * WIDTH])
        bqs = sb("bqs", [P, 1])
        ident = sb("ident", [P, P])
        identb = sb("identb", [P, P], BF16)
        minus_half = sb("minus_half", [P, TILES])
        ones = sb("ones", [1, P])
        gate_sb = sb("gate_sb", [P, EXPERTS])
        down_sb = sb("down_sb", [P, EXPERTS, HIDDEN])
        up_sb = sb("up_sb", [P, EXPERTS, WIDTH])
        downb_sb = sb("downb_sb", [EXPERTS, HIDDEN])
        upb_sb = sb("upb_sb", [EXPERTS, WIDTH])
        iota_sb = sb("iota_sb", [ITEMS, EXPERTS])

        logit = sb("logit", [ITEMS, EXPERTS])
        best = sb("best", [ITEMS, 8])
        nbest = sb("nbest", [ITEMS, 1])
        e = sb("e", [ITEMS, EXPERTS])
        esum = sb("esum", [ITEMS, 1])
        gate = sb("gate", [ITEMS, EXPERTS])
        top = sb("top", [ITEMS, 8])
        which = sb("which", [ITEMS, 8], U32)
        whichf = sb("whichf", [ITEMS, TOP])
        tsum = sb("tsum", [ITEMS, 1])
        wt = sb("wt", [ITEMS, TOP])
        wide = sb("wide", [ITEMS, TOP, HIDDEN])
        hot = sb("hot", [ITEMS, TOP, EXPERTS])
        mix = sb("mix", [ITEMS, EXPERTS])
        weight = sb("weight", [P, ITEMS])
        hotT = sb("hotT", [EXPERTS, TOP + 1, ITEMS])
        biasd = sb("biasd", [P, ITEMS])
        biasu = sb("biasu", [ITEMS, WIDTH])
        biasrow = probs_both[0:1].rearrange("p a b c d -> p (a b c d)")
        index = sb("index", [1, ITEMS * TOP], U32)
        wd = [sb(f"wd{i}", [P, TOP, HIDDEN]) for i in range(2)]
        wu = [sb(f"wu{i}", [P, WIDTH]) for i in range(2)]
        hT = [sb(f"hT{i}", [P, TOKENS]) for i in range(2)]

        scratch = {m: [nc.dram_tensor(f"scratch{m}{i}", [2 * ALL_SLOTS, P, TOKENS], BF16, kind="Internal").ap() for i in range(2)]
                   for m in range(2)}
        tail_in = sem("tail_in")

        def constant_rows(sp, m):
            for D in scratch[m]:
                for qk in range(2):
                    for at in range(SLOTS, ALL_SLOTS):
                        src = tail_c[m, (at - SLOTS) * HEAD:(at - SLOTS + 1) * HEAD, qk, :].unsqueeze(1).broadcast_to([HEAD, PAIRS, TOKENS])
                        for par in range(2):
                            dst = D[ALL_SLOTS * qk + at].rearrange("(x d j) t -> x d j t", x=2, d=HEAD)[par]
                            sp.dma_start(dst, src).then_inc(tail_in, 16)

        banks = [ctx.enter_context(nc.psum_tensor(f"bank{i}", [P, 512], FP32)) for i in range(8)]
        s_bank, t_bank, o_bank, m_bank = banks[0:2], banks[2:4], banks[4:6], banks[6:8]

        x_dram = x_in.rearrange("b (t p) d -> p (b t) d", p=P)
        out_dram = out.rearrange("b (t p) d -> p (b t) d", p=P)

        apart = {}

        def wait_apart(engine, signal, value):
            if not isinstance(value, int):
                if engine.engine not in apart:
                    apart[engine.engine] = engine.alloc_register("apart")
                register = apart[engine.engine]
                engine.reg_mov(register, value)
                value = engine.snap(register)
            engine.wait_ge(x_in_sem, 64)
            engine.wait_ge(signal, value)

        consts_in = sem("consts_in")
        x_in_sem = sem("x_in_sem")
        set_up = sem("set_up")
        with nc.Block() as block:

            @block.sync
            def _(sp):
                for i in range(4):
                    n = ITEMS * TILES // 4
                    sp.dma_start(x[:, i * n:(i + 1) * n, :], x_dram[:, i * n:(i + 1) * n, :]).then_inc(x_in_sem, 16)
                sp.wait_ge(x_in_sem, 64)

            @block.scalar
            def _(act):
                loads = [(wa[:, :], attn_w[:, :]), (wb[:, :], attn_b[:, :]), (ident[:, :], ident_c[:, :]), (gate_sb[:, :], gate_w[:, :]),
                         (down_sb[:, :, :], down_w[:, :, :]), (upb_sb[:, :], up_b[:, :]), (downb_sb[:, :], down_b[:, :]),
                         (iota_sb[:, :], iota_c[:, :])]
                loads += [(up_sb[HIDDEN * k:HIDDEN * (k + 1), :, :], up_w[:, :, :]) for k in range(TOP)]
                for dst, src in loads:
                    act.dma_start(dst, src).then_inc(consts_in, 16)
                act.wait_ge(consts_in, 16 * len(loads))
                nc.scalar.mul(bqs[:, :], wa[:, 512:513], float(HEAD) ** -0.5)
                nc.scalar.copy(identb[:, :], ident[:, :])

            @block.gpsimd
            def _(pool):
                nc.gpsimd.memset(minus_half[:, :], -0.5)
                nc.gpsimd.memset(ones[:, :], 1.0)
                for r in range(RING):
                    nc.gpsimd.memset(values[r][:, :, :, HEAD + 1:], 0.0)
                    nc.gpsimd.memset(values[r][:, :, :, HEAD:HEAD + 1], 1.0)

            @block.vector
            def _(dve):
                for r in range(RING):
                    for par in range(2):
                        others = k_stack[r][BLOCK * (1 - par):BLOCK * (2 - par), :, par, :]
                        nc.vector.memset(others.bitcast(FP32), 0.0)

        def attention(name, w, bias, scale, masked):
            BACK, AHEAD, LOOP0 = 2, 5, 4
            ROUNDS = (ITEMS - AHEAD - LOOP0) // RING
            LOOP1 = LOOP0 + ROUNDS * RING

            def s(what):
                return sem(f"{name}_{what}")

            raw_done, mv_done = s("raw_done"), s("mv_done")
            var_done, rstd_done, xn_ready = s("var_done"), s("rstd_done"), s("xn_ready")
            xT_done, xnT_ready = s("xT_done"), s("xnT_ready")
            qk_done, qk32_ready, hi_ready = s("qk_done"), s("qk32_ready"), s("hi_ready")
            v_done, v_ready = s("v_done"), s("v_ready")
            rest_done, mid_done, parts_ready = s("rest_done"), s("mid_done"), s("parts_ready")
            bounced = [s(f"bounced{i}") for i in range(2)]
            stack_in = [s(f"stack_in{i}") for i in range(2)]
            s_done, max_done = s("s_done"), s("max_done")
            mhi_done, mrest_done, mmid_done, mparts_ready = s("mhi_done"), s("mrest_done"), s("mmid_done"), s("mparts_ready")
            mT_done, maxT_ready = s("mT_done"), s("maxT_ready")
            max_in = [s(f"max_in{i}") for i in range(2)]
            t_done, exp_done = s("t_done"), s("exp_done")
            pv_done, oT_ready = s("pv_done"), s("oT_ready")
            on_done = [s(f"on_done{t}") for t in range(TILES)]
            rsum_done, o_ready = s("rsum_done"), s("o_ready")
            oT2_done, onT_ready = s("oT2_done"), s("onT_ready")
            wo_done, x_ready = s("wo_done"), s("x_ready")
            raw2, mv2, var2, rstd2, yn_ready = s("raw2"), s("mv2"), s("var2"), s("rstd2"), s("yn_ready")
            yT_done, yT_ready = s("yT_done"), s("yT_ready")

            wq, wk, wv, wo = (w[:, i * WIDTH:(i + 1) * WIDTH] for i in range(4))

            def steps(engine, emit):
                def peeled(n):
                    emit(n, n % RING, lambda k: 0 <= n + k < ITEMS, lambda k: (n + k) // 2)
                for n in range(-AHEAD, LOOP0):
                    peeled(n)
                with engine.Fori(0, ROUNDS) as i:
                    for u in range(RING):
                        emit(i * RING + (LOOP0 + u), (LOOP0 + u) % RING, lambda k: True,
                             lambda k: i * (RING // 2) + (LOOP0 + u + k) // 2)
                for n in range(LOOP1, ITEMS + BACK):
                    peeled(n)

            def tiles_of(item):
                return bass.ds(item * TILES, TILES)

            def tile_of(item, t):
                return bass.ds(item * TILES + t, 1)

            with nc.Block() as block:

                @block.sync
                def _(sp):
                    if masked:
                        constant_rows(sp, 0)
                    sp.wait_ge(tail_in, 16 * 16 if masked else 2 * 16 * 16)

                    def step(n, r, live, half):
                        if live(3):
                            D = scratch[0 if masked else 1][(r + 3) % 2]
                            sp.wait_ge(bounced[(r + 3) % 2], half(3) * 96 + 96)
                            if live(-1):
                                sp.wait_ge(t_done, (n - 1) * HEADS + HEADS)
                            for par in range(2):
                                rows = slice(BLOCK * par, BLOCK * (par + 1))
                                q_src, k_src = (D[ALL_SLOTS * qk:ALL_SLOTS * (qk + 1)].rearrange("s (x d j) t -> s x d (j t)", x=2, d=HEAD)[:, par]
                                                for qk in range(2))
                                sp.dma_start(q_stack[(r + 3) % RING][rows, :, :].rearrange("p j t -> p (j t)"),
                                             q_src).then_inc(stack_in[(r + 3) % 2], 16)
                                sp.dma_start(k_stack[(r + 3) % RING][rows, :, par, :], k_src).then_inc(stack_in[(r + 3) % 2], 16)
                        if live(1):
                            sp.wait_ge(maxT_ready, (n + 1) + 1)
                            for par in range(2):
                                dst = q_stack[(r + 1) % RING][BLOCK * par + MAX_ROW:BLOCK * par + MAX_ROW + 3, :, :]
                                sp.dma_start(dst, maxT[(r + 1) % 2][3 * PAIRS * par:3 * PAIRS * (par + 1), :]).then_inc(max_in[(r + 1) % 2], 16)
                        if live(4):
                            D, i = scratch[0 if masked else 1][(r + 4) % 2], (r + 4) % 2
                            sp.wait_ge(parts_ready, (n + 4) + 1)
                            if live(2):
                                sp.wait_ge(stack_in[(r + 2) % 2], half(2) * 64 + 64)
                            at = 0
                            for part in range(3):
                                count = Q_PARTS.count(part)
                                q_src = parts[i][:, part, 0].unsqueeze(1).broadcast_to([P, count, TOKENS])
                                sp.dma_start(D[at:at + count].rearrange("s p t -> p s t"), q_src).then_inc(bounced[(r + 4) % 2], 16)
                                k_src = parts[i][:, 0:count, 1]
                                sp.dma_start(D[ALL_SLOTS + at:ALL_SLOTS + at + count].rearrange("s p t -> p s t"), k_src).then_inc(bounced[(r + 4) % 2], 16)
                                at += count
                    steps(sp, step)

                @block.gpsimd
                def _(pool):
                    def split(src, tmp, hi, mid, lo, hi_done, rest_d, mid_d, lo_d, item):
                        pool.wait_ge(hi_done, item + 1)
                        nc.gpsimd.tensor_tensor(tmp, src, hi, ALU.subtract).then_inc(rest_d, 1)
                        wait_apart(pool, rest_d, item + 1)
                        nc.gpsimd.tensor_scalar(mid, tmp, 1.0, 0.0, ALU.mult, ALU.add).then_inc(mid_d, 1)
                        pool.wait_ge(mid_d, item + 1)
                        nc.gpsimd.tensor_tensor(lo, tmp, mid, ALU.subtract).then_inc(lo_d, 1)

                    def inverse_deviation(item, i, mv_d, var_d, rstd_d):
                        wait_apart(pool, mv_d, item + 1)
                        nc.gpsimd.tensor_scalar(varp[i][:, :], mv[i][:, :, 1], 1.0, EPS, ALU.mult, ALU.add).then_inc(var_d, 1)
                        pool.wait_ge(var_d, item + 1)
                        nc.gpsimd.tensor_tensor(rstd[i][:, :], varp[i][:, :], minus_half[:, :], ALU.pow).then_inc(rstd_d, 1)

                    def step(n, r, live, half):
                        if live(1):
                            i = (r + 1) % 2
                            if live(-1):
                                pool.wait_ge(mT_done, (n - 1) + 1)
                            wait_apart(pool, max_done, (n + 1) * HEADS + HEADS)
                            src = nmax[i][:, :, :].rearrange("p t (x j) -> p (t x) j", x=2)
                            tmp = mrest[i][:, :].rearrange("p (a j) -> p a j", j=PAIRS)
                            nc.gpsimd.tensor_scalar(mparts[i][:, :, 0, :], src, 1.0, 0.0, ALU.mult, ALU.add).then_inc(mhi_done, 1)
                            split(src, tmp, mparts[i][:, :, 0, :], mparts[i][:, :, 1, :], mparts[i][:, :, 2, :],
                                  mhi_done, mrest_done, mmid_done, mparts_ready, n + 1)
                        if live(4):
                            i = (r + 4) % 2
                            pool.wait_ge(qk32_ready, (n + 4) + 1)
                            split(qk32[i][:, :, :], rest[i][:, :, :], parts[i][:, 0], parts[i][:, 1], parts[i][:, 2],
                                  hi_ready, rest_done, mid_done, parts_ready, n + 4)
                        if live(5):
                            inverse_deviation(n + 5, (r + 5) % 2, mv_done, var_done, rstd_done)
                        if live(-2):
                            inverse_deviation(n - 2, 2 + r % 2, mv2, var2, rstd2)
                    steps(pool, step)

                @block.vector
                def _(dve):
                    def stats(item, i, raw_d, mv_d):
                        for t in range(TILES):
                            last = nc.vector.bn_stats(raw[i][:, t, :], x[:, tile_of(item, t), :])
                        last.then_inc(raw_d, 1)

                    def aggregate(item, i, raw_d, mv_d):
                        wait_apart(dve, raw_d, item + 1)
                        for t in range(TILES):
                            last = nc.vector.bn_aggr(mv[i][:, t, :], raw[i][:, t, :])
                        last.then_inc(mv_d, 1)

                    def normalise(item, i, dst, rstd_d, dst_d):
                        dve.wait_ge(rstd_d, item + 1)
                        for t in range(TILES):
                            last = nc.vector.tensor_scalar(dst[:, t:t + 1, :], x[:, tile_of(item, t), :], mv[i][:, t, 0:1],
                                                           rstd[i][:, t:t + 1], ALU.subtract, ALU.mult)
                        last.then_inc(dst_d, 1)

                    def step(n, r, live, half):
                        for p in range(PAIRS):
                            if live(2):
                                i = (r + 2) % 2
                                if p == 0 and live(0):
                                    dve.wait_ge(mparts_ready, n + 1)
                                for t in range(TILES):
                                    dve.wait_ge(s_done, (n + 2) * HEADS + (2 * p + t + 1))
                                    src = s_bank[t][:, :].rearrange("p (x k) -> p x k", x=2)
                                    dst = nmax[i][:, t, :].rearrange("p (x j) -> p x j", x=2)[:, :, p:p + 1]
                                    nc.vector.tensor_reduce(dst, src, axis=AX.X, op=ALU.max, negate=True).then_inc(max_done, 1)
                            if p == 0 and live(5):
                                stats(n + 5, (r + 5) % 2, raw_done, mv_done)
                            if p == 1 and live(5):
                                aggregate(n + 5, (r + 5) % 2, raw_done, mv_done)
                            if p == 5 and live(5):
                                if live(3):
                                    dve.wait_ge(xT_done, (n + 3) + 1)
                                normalise(n + 5, (r + 5) % 2, xn[(r + 5) % 2], rstd_done, xn_ready)
                            if live(-1) and p in (2, 4):
                                t = (1, 0)[p // 4]
                                bank = m_bank[1] if t == 1 else m_bank[0]
                                dve.wait_ge(on_done[t], (n - 1) + 1)
                                both = bank[:, :].rearrange("p (h c) -> p h c", c=32)
                                if live(-2):
                                    dve.wait_ge(oT2_done, (n - 2) + 1)
                                k = 0 if t == 1 else 1
                                nc.vector.reciprocal(rsum[:, t, :], both[:, :, HEAD]).then_inc(rsum_done, 1)
                                dve.wait_ge(rsum_done, (n - 1) * TILES + k + 1)
                                nc.vector.tensor_tensor(o[:, t, :].rearrange("p (h d) -> p h d", d=HEAD), both[:, :, 0:HEAD],
                                                        rsum[:, t, :].unsqueeze(2).broadcast_to([P, HEADS, HEAD]),
                                                        ALU.mult).then_inc(o_ready, 1)
                            if p == 6 and live(-1):
                                dve.wait_ge(wo_done, (n - 1) + 1)
                                xs = x[:, tiles_of(n - 1), :]
                                nc.vector.tensor_tensor(xs, xs, m_bank[1][:, 0:TOKENS].rearrange("p (t d) -> p t d", t=TILES),
                                                        ALU.add).then_inc(x_ready, 1)
                            if p == 3 and live(-2):
                                wait_apart(dve, x_ready, (n - 2) + 1)
                                stats(n - 2, 2 + r % 2, raw2, mv2)
                            if p == 4 and live(-2):
                                aggregate(n - 2, 2 + r % 2, raw2, mv2)
                            if p == 5 and live(-2):
                                if live(-4):
                                    dve.wait_ge(yT_done, (n - 4) + 1)
                                normalise(n - 2, 2 + r % 2, yn[r % 2], rstd2, yn_ready)
                    steps(dve, step)

                @block.scalar
                def _(act):
                    def step(n, r, live, half):
                        for p in range(PAIRS):
                            if live(0):
                                for h in (2 * p, 2 * p + 1):
                                    g, c = divmod(h, PER_GROUP)
                                    if c == 0 and g >= 2:
                                        act.wait_ge(pv_done, n * GROUPS + (g - 1))
                                    elif c == 0 and live(-1):
                                        act.wait_ge(pv_done, (n - 1) * GROUPS + (g + 3))
                                    act.wait_ge(t_done, n * HEADS + (h + 1))
                                    nc.scalar.activation(probs[g % 2][:, c, :, :], t_bank[h % 2][:, :].rearrange("p (k q) -> p k q", k=TILES),
                                                         ACT.Exp).then_inc(exp_done, 1)

                            def values_out(item, i, g):
                                act.wait_ge(pv_done, item * GROUPS + (g + 1))
                                nc.scalar.copy(oT[i][:, g, :], o_bank[g % 2][:, 0:TOKENS]).then_inc(oT_ready, 1)

                            if p == 0 and live(-1):
                                values_out(n - 1, (r - 1) % 2, 3)
                            if p == 0 and live(4):
                                act.wait_ge(xT_done, (n + 4) + 1)
                                nc.scalar.copy(xnT[(r + 4) % 2][:, :], m_bank[0][:, 0:TOKENS]).then_inc(xnT_ready, 1)
                            if p == 0 and live(1):
                                act.wait_ge(mT_done, (n + 1) + 1)
                                if live(-1):
                                    act.wait_ge(max_in[(r - 1) % 2], half(-1) * 32 + 32)
                                nc.scalar.copy(maxT[(r + 1) % 2][:, :],
                                               m_bank[1][:, :].bitcast(BF16)[0:6 * PAIRS, 0:TOKENS]).then_inc(maxT_ready, 1)
                            if p == 1 and live(4):
                                i = (r + 4) % 2
                                act.wait_ge(qk_done, (n + 4) + 1)
                                if live(2):
                                    act.wait_ge(parts_ready, (n + 2) + 1)
                                    act.wait_ge(bounced[(r + 2) % 2], half(2) * 96 + 96)
                                src = m_bank[0][:, :].rearrange("p (a t) -> p a t", a=2)
                                for dst, signal in ((qk32[i], qk32_ready), (parts[i][:, 0], hi_ready)):
                                    if bias:
                                        nc.scalar.activation(dst[:, 0, :], src[:, 0, :], ACT.Identity, bias=bqs[:, :], scale=scale)
                                        last = nc.scalar.activation(dst[:, 1, :], src[:, 1, :], ACT.Identity, bias=w[:, 513:514])
                                    else:
                                        nc.scalar.mul(dst[:, 0, :], src[:, 0, :], scale)
                                        last = nc.scalar.copy(dst[:, 1, :], src[:, 1, :])
                                    last.then_inc(signal, 1)
                            if p == 2 and live(0):
                                values_out(n, r % 2, 0)
                            if p == 2 and live(3):
                                act.wait_ge(v_done, (n + 3) + 1)
                                if live(-1):
                                    act.wait_ge(pv_done, (n - 1) * GROUPS + 4)
                                nc.scalar.copy(values[(r + 3) % RING][:, :, :, 0:HEAD].rearrange("p t h d -> p (t h) d"),
                                               m_bank[0][:, 0:TOKENS].rearrange("p (a d) -> p a d", d=HEAD)).then_inc(v_ready, 1)
                            if p == 4 and live(0):
                                values_out(n, r % 2, 1)
                            if p == 5 and live(-1):
                                act.wait_ge(oT2_done, (n - 1) + 1)
                                if live(-2):
                                    act.wait_ge(wo_done, (n - 2) + 1)
                                if bias:
                                    last = nc.scalar.activation(onT[:, :], m_bank[1][:, 0:TOKENS], ACT.Identity, bias=w[:, 514:515])
                                else:
                                    last = nc.scalar.copy(onT[:, :], m_bank[1][:, 0:TOKENS])
                                last.then_inc(onT_ready, 1)
                            if p == 6 and live(0):
                                values_out(n, r % 2, 2)
                            if p == 7 and live(-2):
                                act.wait_ge(yT_done, (n - 2) + 1)
                                nc.scalar.activation(normT[:, bass.ds(n - 2, 1), :], m_bank[0][:, 0:TOKENS].unsqueeze(1), ACT.Copy,
                                                     accum_out=pooled[:, bass.ds(n - 2, 1)]).then_inc(yT_ready, 1)
                    steps(act, step)

                @block.tensor
                def _(pe):
                    def weigh(item, r, g):
                        pe.wait_ge(exp_done, item * HEADS + PER_GROUP * (g + 1))
                        for k in range(TILES):
                            for c in range(PER_GROUP):
                                last = nc.tensor.matmul(o_bank[g % 2][32 * c:32 * (c + 1), 0:TOKENS],
                                                        values[r % RING][:, k, PER_GROUP * g + c, :], probs[g % 2][:, c, k, :],
                                                        start=(k == 0), stop=(k == TILES - 1))
                        last.then_inc(pv_done, 1)

                    def transpose_sums(item, i, t, bank):
                        for g in range(GROUPS):
                            last = nc.tensor.transpose(bank[:, g * P:(g + 1) * P], oT[i][:, g, t * P:(t + 1) * P], ident[:, :])
                        last.then_inc(on_done[t], 1)

                    def step(n, r, live, half):
                        for p in range(PAIRS):
                            if live(0):
                                if p == 0:
                                    pe.wait_ge(max_in[r % 2], half(0) * 32 + 32)
                                for k in range(TILES):
                                    for h in (2 * p, 2 * p + 1):
                                        if k == 0 and h >= 2:
                                            pe.wait_ge(exp_done, n * HEADS + (h - 1))
                                        elif k == 0 and live(-1):
                                            pe.wait_ge(exp_done, (n - 1) * HEADS + (h + 15))
                                        last = nc.tensor.matmul(t_bank[h % 2][:, k * TOKENS:(k + 1) * TOKENS],
                                                                k_stack[r][:, p, h % 2, k * P:(k + 1) * P], q_stack[r][:, p, :],
                                                                start=(k == 0), stop=(k == TILES - 1))
                                        if k == TILES - 1:
                                            last.then_inc(t_done, 1)
                            if live(2):
                                z = (r + 2) % RING
                                if p == 0:
                                    pe.wait_ge(stack_in[(r + 2) % 2], half(2) * 64 + 64)
                                for t in range(TILES):
                                    use = 2 * p + t
                                    if use >= 2:
                                        pe.wait_ge(max_done, (n + 2) * HEADS + (use - 1))
                                    elif live(1):
                                        pe.wait_ge(max_done, (n + 1) * HEADS + (use + 15))
                                    nc.tensor.matmul(s_bank[t][:, :], q_stack[z][:, p, t * P:(t + 1) * P],
                                                     k_stack[z][:, p, :, :].rearrange("p x t -> p (x t)"),
                                                     start=True, stop=True).then_inc(s_done, 1)
                            if p == 0 and live(-1):
                                if live(-1):
                                    pe.wait_ge(oT_ready, (n - 1) * GROUPS + 2)
                                weigh(n - 1, r - 1, 3)
                            if p == 0 and live(4):
                                pe.wait_ge(xn_ready, (n + 4) + 1)
                                if live(-3):
                                    pe.wait_ge(yT_ready, (n - 3) + 1)
                                if live(-2):
                                    pe.wait_ge(o_ready, (n - 2) * TILES + 2)
                                elif live(2):
                                    pe.wait_ge(v_ready, (n + 2) + 1)
                                if live(3):
                                    pe.wait_ge(hi_ready, (n + 3) + 1)
                                for t in range(TILES):
                                    last = nc.tensor.transpose(m_bank[0][:, t * P:(t + 1) * P], xn[(r + 4) % 2][:, t, :], ident[:, :])
                                last.then_inc(xT_done, 1)
                            if p == 0 and live(1):
                                if live(-2):
                                    pe.wait_ge(x_ready, (n - 2) + 1)
                                elif live(0):
                                    pe.wait_ge(maxT_ready, n + 1)
                                wait_apart(pe, mparts_ready, (n + 1) + 1)
                                for t in range(TILES):
                                    last = nc.tensor.transpose(m_bank[1][:, :].bitcast(BF16)[0:6 * PAIRS, t * P:(t + 1) * P],
                                                               mparts[(r + 1) % 2][:, 2 * t:2 * t + 2, :, :].rearrange("p a b j -> p (a b j)"),
                                                               identb[:, :])
                                last.then_inc(mT_done, 1)
                            if p == 1 and live(4):
                                pe.wait_ge(xnT_ready, (n + 4) + 1)
                                for a, wmat in enumerate((wq, wk)):
                                    last = nc.tensor.matmul(m_bank[0][:, a * TOKENS:(a + 1) * TOKENS], wmat, xnT[(r + 4) % 2][:, :],
                                                            start=(a == 0), stop=(a == 1), skip_group_check=True)
                                last.then_inc(qk_done, 1)
                            if p == 1 and live(-1):
                                pe.wait_ge(oT_ready, (n - 1) * GROUPS + 4)
                                if live(1):
                                    pe.wait_ge(maxT_ready, (n + 1) + 1)
                                elif live(-2):
                                    pe.wait_ge(x_ready, (n - 2) + 1)
                                transpose_sums(n - 1, (r - 1) % 2, 1, m_bank[1])
                            if p == 2 and live(0):
                                if live(-1):
                                    pe.wait_ge(oT_ready, (n - 1) * GROUPS + 3)
                                weigh(n, r, 0)
                            if p == 2 and live(3):
                                pe.wait_ge(xnT_ready, (n + 3) + 1)
                                if live(4):
                                    pe.wait_ge(hi_ready, (n + 4) + 1)
                                elif live(-2):
                                    pe.wait_ge(o_ready, (n - 2) * TILES + 2)
                                if live(-3):
                                    pe.wait_ge(yT_ready, (n - 3) + 1)
                                for t in range(TILES):
                                    last = nc.tensor.matmul(m_bank[0][:, t * P:(t + 1) * P], xnT[(r + 3) % 2][:, t * P:(t + 1) * P], wv,
                                                            start=(t == 0), stop=(t == TILES - 1), skip_group_check=True)
                                last.then_inc(v_done, 1)
                            if p == 3 and live(-1):
                                if live(3):
                                    pe.wait_ge(v_ready, (n + 3) + 1)
                                elif live(-2):
                                    pe.wait_ge(o_ready, (n - 2) * TILES + 2)
                                if live(-3):
                                    pe.wait_ge(yT_ready, (n - 3) + 1)
                                transpose_sums(n - 1, (r - 1) % 2, 0, m_bank[0])
                            if p == 4 and live(0):
                                if live(-1):
                                    pe.wait_ge(oT_ready, (n - 1) * GROUPS + 4)
                                weigh(n, r, 1)
                            if p == 4 and live(-1):
                                pe.wait_ge(o_ready, (n - 1) * TILES + 2)
                                for t in range(TILES):
                                    last = nc.tensor.transpose(m_bank[1][:, t * P:(t + 1) * P], o[:, t, :], ident[:, :])
                                last.then_inc(oT2_done, 1)
                            if p == 5 and live(-1):
                                pe.wait_ge(onT_ready, (n - 1) + 1)
                                for t in range(TILES):
                                    last = nc.tensor.matmul(m_bank[1][:, t * P:(t + 1) * P], onT[:, t * P:(t + 1) * P], wo,
                                                            start=(t == 0), stop=(t == TILES - 1), skip_group_check=True)
                                last.then_inc(wo_done, 1)
                            if p == 6 and live(0):
                                pe.wait_ge(oT_ready, n * GROUPS + 1)
                                weigh(n, r, 2)
                            if p == 6 and live(-2):
                                pe.wait_ge(yn_ready, (n - 2) + 1)
                                if live(-1):
                                    pe.wait_ge(o_ready, (n - 1) * TILES + 2)
                                elif live(-3):
                                    pe.wait_ge(yT_ready, (n - 3) + 1)
                                for t in range(TILES):
                                    last = nc.tensor.transpose(m_bank[0][:, t * P:(t + 1) * P], yn[r % 2][:, t, :], ident[:, :])
                                last.then_inc(yT_done, 1)
                    steps(pe, step)

        def feed_forward(name, store):
            def s(what):
                return sem(f"{name}_{what}")

            pe_g, act_g, dve_g, dma_g = s("pe_gate"), s("act_gate"), s("dve_gate"), s("dma_gate")
            with nc.Block() as block:

                @block.tensor
                def _(pe):
                    nc.tensor.matmul(banks[0][0:ITEMS, 0:EXPERTS], pooled[:, :], gate_sb[:, :], start=True, stop=True).then_inc(pe_g, 1)
                    pe.wait_ge(dve_g, 14)
                    nc.tensor.transpose(banks[1][:, 0:ITEMS], wide[:, :, :].rearrange("p a b -> p (a b)"), ident[0:ITEMS, 0:ITEMS])
                    for k in range(TOP):
                        nc.tensor.transpose(banks[2][0:EXPERTS, k * ITEMS:(k + 1) * ITEMS], hot[:, k, :], ident[0:ITEMS, 0:ITEMS])
                    nc.tensor.transpose(banks[2][0:EXPERTS, TOP * ITEMS:(TOP + 1) * ITEMS], mix[:, :], ident[0:ITEMS, 0:ITEMS]).then_inc(pe_g, 1)
                    pe.wait_ge(dve_g, 16)
                    for k in range(TOP):
                        nc.tensor.matmul(banks[3][HIDDEN * k:HIDDEN * (k + 1), 0:ITEMS], downb_sb[:, :], hotT[:, k, :], start=True, stop=True)
                    nc.tensor.matmul(banks[4][0:ITEMS, 0:WIDTH], hotT[:, TOP, :], upb_sb[:, :], start=True, stop=True).then_inc(pe_g, 1)

                @block.scalar
                def _(act):
                    act.wait_ge(dve_g, 3)
                    nc.scalar.activation(e[:, :], logit[:, :], ACT.Exp, bias=nbest[:, :], accum_out=esum[:, :]).then_inc(act_g, 1)

                @block.vector
                def _(dve):
                    count = [0]

                    def link(ins):
                        count[0] += 1
                        ins.then_inc(dve_g, 1)
                        dve.wait_ge(dve_g, count[0])

                    dve.wait_ge(pe_g, 1)
                    link(nc.vector.tensor_scalar(logit[:, :], banks[0][0:ITEMS, 0:EXPERTS], 1.0 / TOKENS, None, ALU.mult))
                    link(nc.vector.max(best[:, :], logit[:, :]))
                    link(nc.vector.tensor_scalar(nbest[:, :], best[:, 0:1], -1.0, None, ALU.mult))
                    dve.wait_ge(act_g, 1)
                    link(nc.vector.reciprocal(tsum[:, :], esum[:, :]))
                    link(nc.vector.tensor_scalar(gate[:, :], e[:, :], tsum[:, :], None, ALU.mult))
                    link(nc.vector.max(top[:, :], gate[:, :]))
                    link(nc.vector.max_index(which[:, :], top[:, :], gate[:, :]))
                    link(nc.vector.tensor_copy(whichf[:, :], which[:, 0:TOP]))
                    link(nc.vector.tensor_scalar(tsum[:, :], top[:, 0:1], top[:, 1:2], 1e-8, ALU.add, ALU.add))
                    link(nc.vector.reciprocal(tsum[:, :], tsum[:, :]))
                    link(nc.vector.tensor_scalar(wt[:, :], top[:, 0:TOP], tsum[:, :], None, ALU.mult))
                    for k in range(TOP):
                        nc.vector.tensor_copy(wide[:, k, :], wt[:, k:k + 1].broadcast_to([ITEMS, HIDDEN]))
                        last = nc.vector.tensor_scalar(hot[:, k, :], iota_sb[:, :], whichf[:, k:k + 1], None, ALU.is_equal)
                    link(last)
                    link(nc.vector.tensor_scalar(mix[:, :], hot[:, 0, :], wt[:, 0:1], None, ALU.mult))
                    link(nc.vector.scalar_tensor_tensor(out=mix[:, :], in0=hot[:, 1, :], scalar=wt[:, 1:2], in1=mix[:, :],
                                                        op0=ALU.mult, op1=ALU.add))
                    dve.wait_ge(pe_g, 2)
                    link(nc.vector.tensor_copy(weight[:, :], banks[1][:, 0:ITEMS]))
                    link(nc.vector.tensor_copy(hotT[:, :, :].rearrange("p a b -> p (a b)"), banks[2][0:EXPERTS, 0:(TOP + 1) * ITEMS]))
                    dve.wait_ge(pe_g, 3)
                    link(nc.vector.tensor_copy(biasd[:, :], banks[3][:, 0:ITEMS]))
                    link(nc.vector.tensor_copy(biasu[:, :], banks[4][0:ITEMS, 0:WIDTH]))

                @block.sync
                def _(sp):
                    sp.wait_ge(dve_g, 7)
                    sp.dma_start(index[0:1, :].rearrange("a (n k) -> a n k", k=TOP), which[:, 0:TOP]).then_inc(dma_g, 16)
                    sp.wait_ge(dve_g, 18)
                    sp.dma_start(biasrow[0:1, :], biasu[:, :]).then_inc(dma_g, 16)
                    sp.wait_ge(dma_g, 32)

            wd_ready, wu_ready = s("wd_ready"), s("wu_ready")
            down_done, h_ready, up_done, x_ready, stored = s("down_done"), s("h_ready"), s("up_done"), s("x_ready"), s("stored")
            UNROLL, LOOP0 = 2, 3
            ROUNDS = (ITEMS - 1 - LOOP0) // UNROLL

            def steps(engine, emit):
                def peeled(n):
                    emit(n, n % 2, lambda k: 0 <= n + k < ITEMS)
                for n in range(-1, LOOP0):
                    peeled(n)
                with engine.Fori(0, ROUNDS) as i:
                    for u in range(UNROLL):
                        emit(i * UNROLL + (LOOP0 + u), (LOOP0 + u) % 2, lambda k: True)
                for n in range(LOOP0 + ROUNDS * UNROLL, ITEMS + 1):
                    peeled(n)

            with nc.Block() as block:

                @block.gpsimd
                def _(pool):
                    def step(n, i, live):
                        if live(1):
                            i = (i + 1) % 2
                            if live(-1):
                                pool.wait_ge(down_done, (n - 1) + 1)
                            for k in range(TOP):
                                which_k = pool.value_load(index[0:1, bass.ds((n + 1) * TOP + k, 1)], min_val=0, max_val=EXPERTS - 1)
                                last = nc.gpsimd.tensor_copy(wd[i][:, k:k + 1, :], down_sb[:, bass.ds(which_k, 1), :])
                            last.then_inc(wd_ready, 1)
                    steps(pool, step)

                @block.vector
                def _(dve):
                    def step(n, i, live):
                        if live(1):
                            j = (i + 1) % 2
                            if live(-1):
                                dve.wait_ge(up_done, (n - 1) + 1)
                            for k in range(TOP):
                                half = slice(HIDDEN * k, HIDDEN * (k + 1))
                                which_k = dve.value_load(index[0:1, bass.ds((n + 1) * TOP + k, 1)], min_val=0, max_val=EXPERTS - 1)
                                last = nc.vector.tensor_scalar(wu[j][half, :].unsqueeze(1), up_sb[half, bass.ds(which_k, 1), :],
                                                               weight[half, bass.ds(n + 1, 1)], None, ALU.mult)
                            last.then_inc(wu_ready, 1)
                        if live(-1):
                            dve.wait_ge(up_done, (n - 1) + 1)
                            xs = x[:, bass.ds((n - 1) * TILES, TILES), :]
                            src = banks[4 + (i + 1) % 2][:, 0:TOKENS].rearrange("p (t d) -> p t d", t=TILES)
                            nc.vector.tensor_tensor(xs, xs, src, ALU.add).then_inc(x_ready, 1)
                    steps(dve, step)

                @block.scalar
                def _(act):
                    def step(n, i, live):
                        if live(0):
                            act.wait_ge(down_done, n + 1)
                            if live(-2):
                                act.wait_ge(up_done, (n - 2) + 1)
                            nc.scalar.activation(hT[i][:, :], banks[i][:, 0:TOKENS], ACT.Gelu,
                                                 bias=biasd[:, bass.ds(n, 1)]).then_inc(h_ready, 1)
                    steps(act, step)

                @block.tensor
                def _(pe):
                    def step(n, i, live):
                        if live(0):
                            pe.wait_ge(wd_ready, n + 1)
                            if live(-2):
                                pe.wait_ge(h_ready, (n - 2) + 1)
                            nc.tensor.matmul(banks[i][:, 0:TOKENS], wd[i][:, :, :].rearrange("p a b -> p (a b)"),
                                             normT[:, bass.ds(n, 1), :], start=True, stop=True).then_inc(down_done, 1)
                        if live(-1):
                            j = (i + 1) % 2
                            pe.wait_ge(wu_ready, (n - 1) + 1)
                            pe.wait_ge(h_ready, (n - 1) + 1)
                            if live(-3):
                                pe.wait_ge(x_ready, (n - 3) + 1)
                            acc = banks[4 + j]
                            nc.tensor.matmul(acc[:, 0:TOKENS].rearrange("p (t d) -> p t d", t=TILES), ones[0:1, :],
                                             biasrow[0:1, bass.ds((n - 1) * WIDTH, WIDTH)].unsqueeze(1).broadcast_to([1, TILES, WIDTH]),
                                             start=True, stop=False, skip_group_check=True)
                            for t in range(TILES):
                                last = nc.tensor.matmul(acc[:, t * P:(t + 1) * P], hT[j][:, t * P:(t + 1) * P], wu[j][:, :],
                                                        start=False, stop=(t == TILES - 1), skip_group_check=True)
                            last.then_inc(up_done, 1)
                    steps(pe, step)

                @block.sync
                def _(sp):
                    if not store:
                        constant_rows(sp, 1)
                        sp.wait_ge(tail_in, 2 * 16 * 16)
                    if store:
                        def step(n, i, live):
                            if live(-1):
                                sp.wait_ge(x_ready, (n - 1) + 1)
                                at = bass.ds((n - 1) * TILES, TILES)
                                sp.dma_start(out_dram[:, at, :], x[:, at, :]).then_inc(stored, 16)
                        steps(sp, step)
                        sp.wait_ge(stored, 16 * ITEMS)

        attention("a", wa, True, float(HEAD) ** -0.5, True)
        feed_forward("fa", False)
        attention("b", wb, False, float(WIDTH) ** -0.5, False)
        feed_forward("fb", True)


def kernel(L0_attn_a_x, L0_attn_a_Wq, L0_attn_a_bq, L0_attn_a_Wk, L0_attn_a_bk, L0_attn_a_Wv, L0_attn_a_bv, L0_attn_a_Wo,
           L0_attn_b_w_qkv, L0_attn_b_w_out, L0_ffn_gate_w, L0_ffn_down_w, L0_ffn_down_b, L0_ffn_up_w, L0_ffn_up_b):
    import ml_dtypes
    import concourse.bacc as bacc
    from concourse.bass_utils import run_bass_kernel_spmd

    def heads_last(m):
        m = np.asarray(m)
        return m.reshape(m.shape[0], PAIRS, 2, HEAD).transpose(0, 2, 3, 1).reshape(m.shape[0], WIDTH)

    t = lambda m: np.asarray(m).T
    col = lambda v: np.asarray(v).reshape(1, WIDTH)
    w_qkv = np.asarray(L0_attn_b_w_qkv)
    arrays = {
        "x": np.asarray(L0_attn_a_x),
        "attn_a": np.concatenate([heads_last(t(L0_attn_a_Wq)), heads_last(t(L0_attn_a_Wk)), t(L0_attn_a_Wv), t(L0_attn_a_Wo),
                                  heads_last(col(L0_attn_a_bq)).T, heads_last(col(L0_attn_a_bk)).T, col(L0_attn_a_bv).T], 1),
        "attn_b": np.concatenate([heads_last(w_qkv[:, 0:128]), heads_last(w_qkv[:, 128:256]), w_qkv[:, 256:384],
                                  np.asarray(L0_attn_b_w_out)], 1),
        "gate_w": t(L0_ffn_gate_w),
        "down_w": np.asarray(L0_ffn_down_w).transpose(2, 0, 1),
        "down_b": np.asarray(L0_ffn_down_b),
        "up_w": np.asarray(L0_ffn_up_w).transpose(2, 0, 1),
        "up_b": np.asarray(L0_ffn_up_b),
        "tail": rows_of_constants().astype(ml_dtypes.bfloat16),
        "ident": np.eye(P, dtype=np.float32),
        "iota": np.tile(np.arange(EXPERTS, dtype=np.float32), (ITEMS, 1)),
    }
    arrays = {f"in_{k}": np.ascontiguousarray(v) for k, v in arrays.items()}
    nc = bacc.Bacc("TRN2", target_bir_lowering=False, num_devices=1)
    args = [nc.dram_tensor(k, v.shape, mybir.dt.from_np(v.dtype), kind="ExternalInput").ap() for k, v in arrays.items()]
    out = nc.dram_tensor("out", (ITEMS, TOKENS, WIDTH), FP32, kind="ExternalOutput").ap()
    build(nc, *args, out)
    r = run_bass_kernel_spmd(nc, [arrays], core_ids=[0])
    return r.results[0]["out"]
```

```python
import numpy as np

import concourse.bass as bass
from concourse import mybir
from contextlib import ExitStack

FP32 = mybir.dt.float32
BF16 = mybir.dt.bfloat16
U32 = mybir.dt.uint32
ALU = mybir.AluOpType
ACT = mybir.ActivationFunctionType
AX = mybir.AxisListType

P = 128
ITEMS, TOKENS, WIDTH = 32, 256, 128
TILES = TOKENS // P
HEADS, HEAD = 16, 8
PAIRS = HEADS // 2
EXPERTS, HIDDEN, TOP = 8, 64, 2
EPS = 1e-5
NEG = -1.0e30

Q_PARTS = (0, 0, 0, 1, 1, 2)
K_PARTS = (0, 1, 2, 0, 1, 0)
SLOTS = len(Q_PARTS)
BLOCK = 64
MASK_ROW = SLOTS * HEAD
MAX_ROW = MASK_ROW + 2
ALL_SLOTS = BLOCK // HEAD

RING = 4
GROUPS, PER_GROUP = 4, 4
SHARES, IN_SHARE = 2, 2
SUMS = HEAD + 1


def rows_of_constants():
    tail = np.zeros((2, BLOCK - MASK_ROW, 2, TOKENS), np.float32)
    tail[0, 0, 0, 0] = NEG
    tail[0, 1, 0, TOKENS - 1] = NEG
    tail[:, 0, 1, TOKENS - 1] = 1.0
    tail[:, 1, 1, 0] = 1.0
    tail[:, 2:5, 1, :] = 1.0
    return tail


def build(nc, x_in, attn_w, attn_b, gate_w, down_w, down_b, up_w, up_b, tail_c, ident_c, iota_c, pick_c, out):
    ctx = ExitStack()
    with ctx:
        def sb(name, shape, dt=FP32):
            return ctx.enter_context(nc.sbuf_tensor(name, shape, dt))

        def sem(name):
            return ctx.enter_context(nc.semaphore(name))

        x = sb("x", [P, ITEMS * TILES, WIDTH])
        normT = sb("normT", [P, ITEMS, TOKENS])
        pooled = sb("pooled", [P, ITEMS])
        q_stack = [sb(f"q_stack{r}", [P, PAIRS, TOKENS], BF16) for r in range(RING)]
        k_stack = [sb(f"k_stack{r}", [P, PAIRS, 2, TOKENS], BF16) for r in range(RING)]
        values = [sb(f"values{r}", [P, TILES, HEADS, 32]) for r in range(RING)]
        qk32 = [sb(f"qk32_{i}", [P, 2, TOKENS]) for i in range(2)]
        rest = [sb(f"rest{i}", [P, 2, TOKENS]) for i in range(2)]
        parts = [sb(f"parts{i}", [P, 3, 2, TOKENS], BF16) for i in range(2)]
        probs = [sb(f"probs{i}", [P, PER_GROUP, TILES, TOKENS]) for i in range(2)]
        xn = [sb(f"xn{i}", [P, TILES, WIDTH]) for i in range(2)]
        yn = [sb(f"yn{i}", [P, TILES, WIDTH]) for i in range(2)]
        xnT = [sb(f"xnT{i}", [P, TOKENS]) for i in range(2)]
        raw = [sb(f"raw{i}", [P, TILES, 6]) for i in range(4)]
        mv = [sb(f"mv{i}", [P, TILES, 2]) for i in range(4)]
        varp = [sb(f"varp{i}", [P, TILES]) for i in range(4)]
        rstd = [sb(f"rstd{i}", [P, TILES]) for i in range(4)]
        nmax = [sb(f"nmax{i}", [P, TILES, HEADS]) for i in range(2)]
        mrest = [sb(f"mrest{i}", [P, TILES * HEADS]) for i in range(2)]
        mparts = [sb(f"mparts{i}", [P, TILES * 2, 3, PAIRS], BF16) for i in range(2)]
        maxT = [sb(f"maxT{i}", [2 * 3 * PAIRS, TOKENS], BF16) for i in range(2)]
        oT = [sb(f"oT{i}", [P, SHARES, TOKENS]) for i in range(2)]
        rsum = sb("rsum", [P, TILES * HEADS // IN_SHARE, IN_SHARE])
        o = sb("o", [P, TILES, WIDTH])
        onT = sb("onT", [P, TOKENS])
        wa = sb("wa", [P, 4 * WIDTH + 3])
        wb = sb("wb", [P, 4 * WIDTH])
        bqs = sb("bqs", [P, 1])
        ident = sb("ident", [P, P])
        identb = sb("identb", [P, P], BF16)
        minus_half = sb("minus_half", [P, TILES])
        gate_sb = sb("gate_sb", [P, EXPERTS])
        down_sb = sb("down_sb", [P, EXPERTS, HIDDEN])
        up_sb = sb("up_sb", [P, EXPERTS, WIDTH])
        downb_sb = sb("downb_sb", [EXPERTS, HIDDEN])
        upb_sb = sb("upb_sb", [EXPERTS, WIDTH])
        iota_sb = sb("iota_sb", [ITEMS, EXPERTS])

        logit = sb("logit", [ITEMS, EXPERTS])
        best = sb("best", [ITEMS, 8])
        nbest = sb("nbest", [ITEMS, 1])
        e = sb("e", [ITEMS, EXPERTS])
        esum = sb("esum", [ITEMS, 1])
        gate = sb("gate", [ITEMS, EXPERTS])
        top = sb("top", [ITEMS, 8])
        which = sb("which", [ITEMS, 8], U32)
        whichf = sb("whichf", [ITEMS, TOP])
        tsum = sb("tsum", [ITEMS, 1])
        wt = sb("wt", [ITEMS, TOP])
        wide = sb("wide", [ITEMS, TOP, HIDDEN])
        hot = sb("hot", [ITEMS, TOP, EXPERTS])
        mix = sb("mix", [ITEMS, EXPERTS])
        weight = sb("weight", [P, ITEMS])
        hotT = sb("hotT", [EXPERTS, TOP + 3, ITEMS])
        biasd = sb("biasd", [P, ITEMS])
        biasu = sb("biasu", [3 * ITEMS, WIDTH])
        biasu_rest = sb("biasu_rest", [3 * ITEMS, WIDTH])
        biasu_mid = sb("biasu_mid", [3 * ITEMS, WIDTH], BF16)
        biasu_parts = sb("biasu_parts", [3 * ITEMS, WIDTH], BF16)
        pick = sb("pick", [3 * ITEMS, ITEMS], BF16)
        index = sb("index", [1, ITEMS * TOP], U32)
        wd = [sb(f"wd{i}", [P, TOP, HIDDEN]) for i in range(RING)]
        wu = [sb(f"wu{i}", [P, WIDTH]) for i in range(RING)]
        hT = [sb(f"hT{i}", [P, TOKENS]) for i in range(2)]

        scratch = {m: [nc.dram_tensor(f"scratch{m}{i}", [2 * ALL_SLOTS, P, TOKENS], BF16, kind="Internal").ap() for i in range(2)]
                   for m in range(2)}
        tail_in = sem("tail_in")

        def constant_rows(sp, m):
            for D in scratch[m]:
                for qk in range(2):
                    for at in range(SLOTS, ALL_SLOTS):
                        src = tail_c[m, (at - SLOTS) * HEAD:(at - SLOTS + 1) * HEAD, qk, :].unsqueeze(1).broadcast_to([HEAD, PAIRS, TOKENS])
                        for par in range(2):
                            dst = D[ALL_SLOTS * qk + at].rearrange("(x d j) t -> x d j t", x=2, d=HEAD)[par]
                            sp.dma_start(dst, src).then_inc(tail_in, 16)

        def of_group(r, g):
            return values[r][:, :, :, :].rearrange("p t (b c) w -> p (t b) c w", c=PER_GROUP)[:, g::IN_SHARE]

        banks = [ctx.enter_context(nc.psum_tensor(f"bank{i}", [P, 512], FP32)) for i in range(8)]
        s_bank, t_bank, o_bank, m_bank = banks[0:2], banks[2:4], banks[4:6], banks[6:8]

        x_dram = x_in.rearrange("b (t p) d -> p (b t) d", p=P)
        out_dram = out.rearrange("b (t p) d -> p (b t) d", p=P)

        apart = {}

        def wait_apart(engine, signal, value):
            if not isinstance(value, int):
                if engine.engine not in apart:
                    apart[engine.engine] = engine.alloc_register("apart")
                register = apart[engine.engine]
                engine.reg_mov(register, value)
                value = engine.snap(register)
            engine.wait_ge(x_in_sem, 64)
            engine.wait_ge(signal, value)

        consts_in = sem("consts_in")
        x_in_sem = sem("x_in_sem")
        set_up = sem("set_up")
        with nc.Block() as block:

            @block.sync
            def _(sp):
                for i in range(4):
                    n = ITEMS * TILES // 4
                    sp.dma_start(x[:, i * n:(i + 1) * n, :], x_dram[:, i * n:(i + 1) * n, :]).then_inc(x_in_sem, 16)
                sp.wait_ge(x_in_sem, 64)

            @block.scalar
            def _(act):
                loads = [(wa[:, :], attn_w[:, :]), (wb[:, :], attn_b[:, :]), (ident[:, :], ident_c[:, :]), (gate_sb[:, :], gate_w[:, :]),
                         (down_sb[:, :, :], down_w[:, :, :]), (upb_sb[:, :], up_b[:, :]), (downb_sb[:, :], down_b[:, :]),
                         (iota_sb[:, :], iota_c[:, :]), (pick[:, :], pick_c[:, :])]
                loads += [(up_sb[HIDDEN * k:HIDDEN * (k + 1), :, :], up_w[:, :, :]) for k in range(TOP)]
                for dst, src in loads:
                    act.dma_start(dst, src).then_inc(consts_in, 16)
                act.wait_ge(consts_in, 16 * len(loads))
                nc.scalar.mul(bqs[:, :], wa[:, 512:513], float(HEAD) ** -0.5)
                nc.scalar.copy(identb[:, :], ident[:, :])

            @block.gpsimd
            def _(pool):
                nc.gpsimd.memset(minus_half[:, :], -0.5)
                for r in range(RING):
                    nc.gpsimd.memset(values[r][:, :, :, :], 0.0).then_inc(set_up, 1)
                for r in range(RING):
                    pool.wait_ge(set_up, r + 1)
                    for g in range(IN_SHARE):
                        at = SUMS * g + HEAD
                        nc.gpsimd.memset(of_group(r, g)[:, :, :, at:at + 1], 1.0)

            @block.vector
            def _(dve):
                for r in range(RING):
                    for par in range(2):
                        others = k_stack[r][BLOCK * (1 - par):BLOCK * (2 - par), :, par, :]
                        nc.vector.memset(others.bitcast(FP32), 0.0)

        def attention(name, w, bias, scale, masked):
            BACK, AHEAD, LOOP0 = 2, 5, 4
            ROUNDS = (ITEMS - AHEAD - LOOP0) // RING
            LOOP1 = LOOP0 + ROUNDS * RING

            def s(what):
                return sem(f"{name}_{what}")

            raw_done, mv_done = s("raw_done"), s("mv_done")
            var_done, rstd_done, xn_ready = s("var_done"), s("rstd_done"), s("xn_ready")
            xT_done, xnT_ready = s("xT_done"), s("xnT_ready")
            qk_done, qk32_ready, hi_ready = s("qk_done"), s("qk32_ready"), s("hi_ready")
            v_done, v_ready = s("v_done"), s("v_ready")
            rest_done, mid_done, parts_ready = s("rest_done"), s("mid_done"), s("parts_ready")
            bounced = [s(f"bounced{i}") for i in range(2)]
            stack_in = [s(f"stack_in{i}") for i in range(2)]
            s_done, max_done = s("s_done"), s("max_done")
            mhi_done, mrest_done, mmid_done, mparts_ready = s("mhi_done"), s("mrest_done"), s("mmid_done"), s("mparts_ready")
            mT_done, maxT_ready = s("mT_done"), s("maxT_ready")
            max_in = [s(f"max_in{i}") for i in range(2)]
            t_done, exp_done = s("t_done"), s("exp_done")
            pv_done = s("pv_done")
            oT_ready = s("oT_ready")
            on_done, rsum_done, o_ready = s("on_done"), s("rsum_done"), s("o_ready")
            oT2_done, onT_ready = s("oT2_done"), s("onT_ready")
            wo_done, x_ready = s("wo_done"), s("x_ready")
            raw2, mv2, var2, rstd2, yn_ready = s("raw2"), s("mv2"), s("var2"), s("rstd2"), s("yn_ready")
            yT_done, yT_ready = s("yT_done"), s("yT_ready")

            wq, wk, wv, wo = (w[:, i * WIDTH:(i + 1) * WIDTH] for i in range(4))

            def steps(engine, emit):
                def peeled(n):
                    emit(n, n % RING, lambda k: 0 <= n + k < ITEMS, lambda k: (n + k) // 2)
                for n in range(-AHEAD, LOOP0):
                    peeled(n)
                with engine.Fori(0, ROUNDS) as i:
                    for u in range(RING):
                        emit(i * RING + (LOOP0 + u), (LOOP0 + u) % RING, lambda k: True,
                             lambda k: i * (RING // 2) + (LOOP0 + u + k) // 2)
                for n in range(LOOP1, ITEMS + BACK):
                    peeled(n)

            def tiles_of(item):
                return bass.ds(item * TILES, TILES)

            def tile_of(item, t):
                return bass.ds(item * TILES + t, 1)

            with nc.Block() as block:

                @block.sync
                def _(sp):
                    if masked:
                        constant_rows(sp, 0)
                    sp.wait_ge(tail_in, 16 * 16 if masked else 2 * 16 * 16)

                    def step(n, r, live, half):
                        if live(3):
                            D = scratch[0 if masked else 1][(r + 3) % 2]
                            sp.wait_ge(bounced[(r + 3) % 2], half(3) * 96 + 96)
                            if live(-1):
                                sp.wait_ge(t_done, (n - 1) * HEADS + HEADS)
                            for par in range(2):
                                rows = slice(BLOCK * par, BLOCK * (par + 1))
                                q_src, k_src = (D[ALL_SLOTS * qk:ALL_SLOTS * (qk + 1)].rearrange("s (x d j) t -> s x d (j t)", x=2, d=HEAD)[:, par]
                                                for qk in range(2))
                                sp.dma_start(q_stack[(r + 3) % RING][rows, :, :].rearrange("p j t -> p (j t)"),
                                             q_src).then_inc(stack_in[(r + 3) % 2], 16)
                                sp.dma_start(k_stack[(r + 3) % RING][rows, :, par, :], k_src).then_inc(stack_in[(r + 3) % 2], 16)
                        if live(1):
                            sp.wait_ge(maxT_ready, (n + 1) + 1)
                            for par in range(2):
                                dst = q_stack[(r + 1) % RING][BLOCK * par + MAX_ROW:BLOCK * par + MAX_ROW + 3, :, :]
                                sp.dma_start(dst, maxT[(r + 1) % 2][3 * PAIRS * par:3 * PAIRS * (par + 1), :]).then_inc(max_in[(r + 1) % 2], 16)
                        if live(4):
                            D, i = scratch[0 if masked else 1][(r + 4) % 2], (r + 4) % 2
                            sp.wait_ge(parts_ready, (n + 4) + 1)
                            if live(2):
                                sp.wait_ge(stack_in[(r + 2) % 2], half(2) * 64 + 64)
                            at = 0
                            for part in range(3):
                                count = Q_PARTS.count(part)
                                q_src = parts[i][:, part, 0].unsqueeze(1).broadcast_to([P, count, TOKENS])
                                sp.dma_start(D[at:at + count].rearrange("s p t -> p s t"), q_src).then_inc(bounced[(r + 4) % 2], 16)
                                k_src = parts[i][:, 0:count, 1]
                                sp.dma_start(D[ALL_SLOTS + at:ALL_SLOTS + at + count].rearrange("s p t -> p s t"), k_src).then_inc(bounced[(r + 4) % 2], 16)
                                at += count
                    steps(sp, step)

                @block.gpsimd
                def _(pool):
                    def split(src, tmp, hi, mid, lo, hi_done, rest_d, mid_d, lo_d, item):
                        pool.wait_ge(hi_done, item + 1)
                        nc.gpsimd.tensor_tensor(tmp, src, hi, ALU.subtract).then_inc(rest_d, 1)
                        wait_apart(pool, rest_d, item + 1)
                        nc.gpsimd.tensor_scalar(mid, tmp, 1.0, 0.0, ALU.mult, ALU.add).then_inc(mid_d, 1)
                        pool.wait_ge(mid_d, item + 1)
                        nc.gpsimd.tensor_tensor(lo, tmp, mid, ALU.subtract).then_inc(lo_d, 1)

                    def inverse_deviation(item, i, mv_d, var_d, rstd_d):
                        wait_apart(pool, mv_d, item + 1)
                        nc.gpsimd.tensor_scalar(varp[i][:, :], mv[i][:, :, 1], 1.0, EPS, ALU.mult, ALU.add).then_inc(var_d, 1)
                        pool.wait_ge(var_d, item + 1)
                        nc.gpsimd.tensor_tensor(rstd[i][:, :], varp[i][:, :], minus_half[:, :], ALU.pow).then_inc(rstd_d, 1)

                    def step(n, r, live, half):
                        if live(1):
                            i = (r + 1) % 2
                            if live(-1):
                                pool.wait_ge(mT_done, (n - 1) + 1)
                            wait_apart(pool, max_done, (n + 1) * HEADS + HEADS)
                            src = nmax[i][:, :, :].rearrange("p t (x j) -> p (t x) j", x=2)
                            tmp = mrest[i][:, :].rearrange("p (a j) -> p a j", j=PAIRS)
                            nc.gpsimd.tensor_scalar(mparts[i][:, :, 0, :], src, 1.0, 0.0, ALU.mult, ALU.add).then_inc(mhi_done, 1)
                            split(src, tmp, mparts[i][:, :, 0, :], mparts[i][:, :, 1, :], mparts[i][:, :, 2, :],
                                  mhi_done, mrest_done, mmid_done, mparts_ready, n + 1)
                        if live(5):
                            inverse_deviation(n + 5, (r + 5) % 2, mv_done, var_done, rstd_done)
                        if live(-2):
                            inverse_deviation(n - 2, 2 + r % 2, mv2, var2, rstd2)
                        if live(4):
                            i = (r + 4) % 2
                            pool.wait_ge(qk32_ready, (n + 4) + 1)
                            split(qk32[i][:, :, :], rest[i][:, :, :], parts[i][:, 0], parts[i][:, 1], parts[i][:, 2],
                                  hi_ready, rest_done, mid_done, parts_ready, n + 4)
                    steps(pool, step)

                @block.vector
                def _(dve):
                    def stats(item, i, raw_d, mv_d):
                        for t in range(TILES):
                            last = nc.vector.bn_stats(raw[i][:, t, :], x[:, tile_of(item, t), :])
                        last.then_inc(raw_d, 1)

                    def aggregate(item, i, raw_d, mv_d):
                        wait_apart(dve, raw_d, item + 1)
                        for t in range(TILES):
                            last = nc.vector.bn_aggr(mv[i][:, t, :], raw[i][:, t, :])
                        last.then_inc(mv_d, 1)

                    def normalise(item, i, dst, rstd_d, dst_d):
                        dve.wait_ge(rstd_d, item + 1)
                        for t in range(TILES):
                            last = nc.vector.tensor_scalar(dst[:, t:t + 1, :], x[:, tile_of(item, t), :], mv[i][:, t, 0:1],
                                                           rstd[i][:, t:t + 1], ALU.subtract, ALU.mult)
                        last.then_inc(dst_d, 1)

                    def step(n, r, live, half):
                        for p in range(PAIRS):
                            if live(2):
                                i = (r + 2) % 2
                                if p == 0 and live(0):
                                    dve.wait_ge(mparts_ready, n + 1)
                                for t in range(TILES):
                                    dve.wait_ge(s_done, (n + 2) * HEADS + (2 * p + t + 1))
                                    src = s_bank[t][:, :].rearrange("p (x k) -> p x k", x=2)
                                    dst = nmax[i][:, t, :].rearrange("p (x j) -> p x j", x=2)[:, :, p:p + 1]
                                    nc.vector.tensor_reduce(dst, src, axis=AX.X, op=ALU.max, negate=True).then_inc(max_done, 1)
                            if p == 0 and live(-2):
                                dve.wait_ge(wo_done, (n - 2) + 1)
                                xs = x[:, tiles_of(n - 2), :]
                                nc.vector.tensor_tensor(xs, xs, m_bank[1][:, 0:TOKENS].rearrange("p (t d) -> p t d", t=TILES),
                                                        ALU.add).then_inc(x_ready, 1)
                            if p == 0 and live(5):
                                stats(n + 5, (r + 5) % 2, raw_done, mv_done)
                            if p == 1 and live(5):
                                aggregate(n + 5, (r + 5) % 2, raw_done, mv_done)
                            if p == 5 and live(5):
                                if live(3):
                                    dve.wait_ge(xT_done, (n + 3) + 1)
                                normalise(n + 5, (r + 5) % 2, xn[(r + 5) % 2], rstd_done, xn_ready)
                            if p == 3 and live(-1):
                                dve.wait_ge(on_done, (n - 1) + 1)
                                if live(-2):
                                    dve.wait_ge(oT2_done, (n - 2) + 1)
                                both = m_bank[1][:, :].rearrange("p (m w) -> p m w", w=32)[:, :, 0:IN_SHARE * SUMS]
                                both = both.rearrange("p m (g e) -> p m g e", g=IN_SHARE)
                                nc.vector.reciprocal(rsum[:, :, :], both[:, :, :, HEAD]).then_inc(rsum_done, 1)
                                dve.wait_ge(rsum_done, (n - 1) + 1)
                                nc.vector.tensor_tensor(o[:, :, :].rearrange("p t (m g d) -> p (t m) g d", g=IN_SHARE, d=HEAD),
                                                        both[:, :, :, 0:HEAD], rsum[:, :, :].unsqueeze(3).broadcast_to(
                                                            [P, TILES * HEADS // IN_SHARE, IN_SHARE, HEAD]), ALU.mult).then_inc(o_ready, 1)
                            if p == 2 and live(-2):
                                wait_apart(dve, x_ready, (n - 2) + 1)
                                stats(n - 2, 2 + r % 2, raw2, mv2)
                            if p == 3 and live(-2):
                                aggregate(n - 2, 2 + r % 2, raw2, mv2)
                            if p == 5 and live(-2):
                                if live(-4):
                                    dve.wait_ge(yT_done, (n - 4) + 1)
                                normalise(n - 2, 2 + r % 2, yn[r % 2], rstd2, yn_ready)
                    steps(dve, step)

                @block.scalar
                def _(act):
                    def step(n, r, live, half):
                        for p in range(PAIRS):
                            if live(0):
                                for h in (2 * p, 2 * p + 1):
                                    g, c = divmod(h, PER_GROUP)
                                    if c == 0 and g >= 2:
                                        act.wait_ge(pv_done, n * GROUPS + (g - 1))
                                    elif c == 0 and live(-1):
                                        act.wait_ge(pv_done, (n - 1) * GROUPS + (g + 3))
                                    act.wait_ge(t_done, n * HEADS + (h + 1))
                                    nc.scalar.activation(probs[g % 2][:, c, :, :], t_bank[h % 2][:, :].rearrange("p (k q) -> p k q", k=TILES),
                                                         ACT.Exp).then_inc(exp_done, 1)

                            def values_out(item, i, a):
                                act.wait_ge(pv_done, item * GROUPS + IN_SHARE * (a + 1))
                                nc.scalar.copy(oT[i][:, a, :], o_bank[a][:, 0:TOKENS]).then_inc(oT_ready, 1)

                            if p == 0 and live(4):
                                act.wait_ge(xT_done, (n + 4) + 1)
                                nc.scalar.copy(xnT[(r + 4) % 2][:, :], m_bank[0][:, 0:TOKENS]).then_inc(xnT_ready, 1)
                            if p == 1 and live(-1):
                                values_out(n - 1, (r - 1) % 2, 1)
                            if p == 1 and live(1):
                                act.wait_ge(mT_done, (n + 1) + 1)
                                if live(-1):
                                    act.wait_ge(max_in[(r - 1) % 2], half(-1) * 32 + 32)
                                nc.scalar.copy(maxT[(r + 1) % 2][:, :],
                                               m_bank[1][:, :].bitcast(BF16)[0:6 * PAIRS, 0:TOKENS]).then_inc(maxT_ready, 1)
                            if p in (2, 3) and live(4):
                                i = (r + 4) % 2
                                if p == 2:
                                    act.wait_ge(qk_done, (n + 4) + 1)
                                    if live(2):
                                        act.wait_ge(parts_ready, (n + 2) + 1)
                                        act.wait_ge(bounced[(r + 2) % 2], half(2) * 96 + 96)
                                src = m_bank[0][:, :].rearrange("p (a t) -> p a t", a=2)
                                dst, signal = ((qk32[i], qk32_ready), (parts[i][:, 0], hi_ready))[p - 2]
                                if bias:
                                    nc.scalar.activation(dst[:, 0, :], src[:, 0, :], ACT.Identity, bias=bqs[:, :], scale=scale)
                                    last = nc.scalar.activation(dst[:, 1, :], src[:, 1, :], ACT.Identity, bias=w[:, 513:514])
                                else:
                                    nc.scalar.mul(dst[:, 0, :], src[:, 0, :], scale)
                                    last = nc.scalar.copy(dst[:, 1, :], src[:, 1, :])
                                last.then_inc(signal, 1)
                            if p == 5 and live(0):
                                values_out(n, r % 2, 0)
                            if p == 5 and live(3):
                                act.wait_ge(v_done, (n + 3) + 1)
                                if live(-1):
                                    act.wait_ge(pv_done, (n - 1) * GROUPS + 4)
                                src = m_bank[0][:, 0:TOKENS].rearrange("p (b c d) -> p b c d", c=PER_GROUP, d=HEAD)
                                for g in range(IN_SHARE):
                                    last = nc.scalar.copy(of_group((r + 3) % RING, g)[:, :, :, SUMS * g:SUMS * g + HEAD], src[:, g::IN_SHARE])
                                last.then_inc(v_ready, 1)
                            if p == 6 and live(-1):
                                act.wait_ge(oT2_done, (n - 1) + 1)
                                if live(-2):
                                    act.wait_ge(wo_done, (n - 2) + 1)
                                if bias:
                                    last = nc.scalar.activation(onT[:, :], m_bank[1][:, 0:TOKENS], ACT.Identity, bias=w[:, 514:515])
                                else:
                                    last = nc.scalar.copy(onT[:, :], m_bank[1][:, 0:TOKENS])
                                last.then_inc(onT_ready, 1)
                            if p == 7 and live(-2):
                                act.wait_ge(yT_done, (n - 2) + 1)
                                nc.scalar.activation(normT[:, bass.ds(n - 2, 1), :], m_bank[0][:, 0:TOKENS].unsqueeze(1), ACT.Copy,
                                                     accum_out=pooled[:, bass.ds(n - 2, 1)]).then_inc(yT_ready, 1)
                    steps(act, step)

                @block.tensor
                def _(pe):
                    def weigh(item, r, g):
                        pe.wait_ge(exp_done, item * HEADS + PER_GROUP * (g + 1))
                        a, g2 = divmod(g, IN_SHARE)
                        for k in range(TILES):
                            for c in range(PER_GROUP):
                                last = nc.tensor.matmul(o_bank[a][32 * c:32 * (c + 1), 0:TOKENS],
                                                        values[r % RING][:, k, PER_GROUP * g + c, :], probs[g % 2][:, c, k, :],
                                                        start=(g2 == 0 and k == 0), stop=(g2 == IN_SHARE - 1 and k == TILES - 1),
                                                        skip_group_check=True)
                        last.then_inc(pv_done, 1)

                    def step(n, r, live, half):
                        for p in range(PAIRS):
                            z = (r + 2) % RING
                            if p == 0 and live(0):
                                pe.wait_ge(max_in[r % 2], half(0) * 32 + 32)
                            if p == 0 and live(2):
                                pe.wait_ge(stack_in[(r + 2) % 2], half(2) * 64 + 64)
                            for a in range(2):
                                h = 2 * p + a
                                if live(0):
                                    if h >= 2:
                                        pe.wait_ge(exp_done, n * HEADS + (h - 1))
                                    elif live(-1):
                                        pe.wait_ge(exp_done, (n - 1) * HEADS + (h + 15))
                                    for k in range(TILES):
                                        last = nc.tensor.matmul(t_bank[a][:, k * TOKENS:(k + 1) * TOKENS],
                                                                k_stack[r][:, p, a, k * P:(k + 1) * P], q_stack[r][:, p, :],
                                                                start=(k == 0), stop=(k == TILES - 1))
                                    last.then_inc(t_done, 1)
                                if live(2):
                                    if h >= 2:
                                        pe.wait_ge(max_done, (n + 2) * HEADS + (h - 1))
                                    elif live(1):
                                        pe.wait_ge(max_done, (n + 1) * HEADS + (h + 15))
                                    nc.tensor.matmul(s_bank[a][:, :], q_stack[z][:, p, a * P:(a + 1) * P],
                                                     k_stack[z][:, p, :, :].rearrange("p x t -> p (x t)"),
                                                     start=True, stop=True).then_inc(s_done, 1)
                            if p == 0 and live(-1):
                                weigh(n - 1, r - 1, 3)
                            if p == 0 and live(4):
                                pe.wait_ge(xn_ready, (n + 4) + 1)
                                if live(-3):
                                    pe.wait_ge(yT_ready, (n - 3) + 1)
                                elif live(2):
                                    pe.wait_ge(v_ready, (n + 2) + 1)
                                elif live(3):
                                    pe.wait_ge(hi_ready, (n + 3) + 1)
                                for t in range(TILES):
                                    last = nc.tensor.transpose(m_bank[0][:, t * P:(t + 1) * P], xn[(r + 4) % 2][:, t, :], ident[:, :])
                                last.then_inc(xT_done, 1)
                            if p == 1 and live(1):
                                if live(-2):
                                    pe.wait_ge(x_ready, (n - 2) + 1)
                                elif live(0):
                                    pe.wait_ge(maxT_ready, n + 1)
                                wait_apart(pe, mparts_ready, (n + 1) + 1)
                                for t in range(TILES):
                                    last = nc.tensor.transpose(m_bank[1][:, :].bitcast(BF16)[0:6 * PAIRS, t * P:(t + 1) * P],
                                                               mparts[(r + 1) % 2][:, 2 * t:2 * t + 2, :, :].rearrange("p a b j -> p (a b j)"),
                                                               identb[:, :])
                                last.then_inc(mT_done, 1)
                            if p == 1 and live(4):
                                pe.wait_ge(xnT_ready, (n + 4) + 1)
                                for a, wmat in enumerate((wq, wk)):
                                    last = nc.tensor.matmul(m_bank[0][:, a * TOKENS:(a + 1) * TOKENS], wmat, xnT[(r + 4) % 2][:, :],
                                                            start=(a == 0), stop=(a == 1), skip_group_check=True)
                                last.then_inc(qk_done, 1)
                            if p == 2 and live(0):
                                if live(-1):
                                    pe.wait_ge(oT_ready, (n - 1) * SHARES + 1)
                                weigh(n, r, 0)
                            if p == 3 and live(-1):
                                pe.wait_ge(oT_ready, (n - 1) * SHARES + 2)
                                if live(1):
                                    pe.wait_ge(maxT_ready, (n + 1) + 1)
                                elif live(-2):
                                    pe.wait_ge(x_ready, (n - 2) + 1)
                                for t in range(TILES):
                                    for a in range(SHARES):
                                        at = (t * SHARES + a) * P
                                        last = nc.tensor.transpose(m_bank[1][:, at:at + P], oT[(r - 1) % 2][:, a, t * P:(t + 1) * P], ident[:, :])
                                last.then_inc(on_done, 1)
                            if p == 4 and live(0):
                                weigh(n, r, 1)
                            if p == 4 and live(3):
                                pe.wait_ge(xnT_ready, (n + 3) + 1)
                                if live(4):
                                    pe.wait_ge(hi_ready, (n + 4) + 1)
                                elif live(-3):
                                    pe.wait_ge(yT_ready, (n - 3) + 1)
                                for t in range(TILES):
                                    last = nc.tensor.matmul(m_bank[0][:, t * P:(t + 1) * P], xnT[(r + 3) % 2][:, t * P:(t + 1) * P], wv,
                                                            start=(t == 0), stop=(t == TILES - 1), skip_group_check=True)
                                last.then_inc(v_done, 1)
                            if p == 5 and live(-1):
                                pe.wait_ge(o_ready, (n - 1) + 1)
                                for t in range(TILES):
                                    last = nc.tensor.transpose(m_bank[1][:, t * P:(t + 1) * P], o[:, t, :], ident[:, :])
                                last.then_inc(oT2_done, 1)
                            if p == 6 and live(0):
                                if live(-1):
                                    pe.wait_ge(oT_ready, (n - 1) * SHARES + 2)
                                weigh(n, r, 2)
                            if p == 6 and live(-2):
                                pe.wait_ge(yn_ready, (n - 2) + 1)
                                if live(3):
                                    pe.wait_ge(v_ready, (n + 3) + 1)
                                elif live(-3):
                                    pe.wait_ge(yT_ready, (n - 3) + 1)
                                for t in range(TILES):
                                    last = nc.tensor.transpose(m_bank[0][:, t * P:(t + 1) * P], yn[r % 2][:, t, :], ident[:, :])
                                last.then_inc(yT_done, 1)
                            if p == 7 and live(-1):
                                pe.wait_ge(onT_ready, (n - 1) + 1)
                                for t in range(TILES):
                                    last = nc.tensor.matmul(m_bank[1][:, t * P:(t + 1) * P], onT[:, t * P:(t + 1) * P], wo,
                                                            start=(t == 0), stop=(t == TILES - 1), skip_group_check=True)
                                last.then_inc(wo_done, 1)
                    steps(pe, step)

        def feed_forward(name, store):
            def s(what):
                return sem(f"{name}_{what}")

            pe_g, act_g, dve_g, index_in = s("pe_gate"), s("act_gate"), s("dve_gate"), s("index_in")
            wd_ready, wu_ready = s("wd_ready"), s("wu_ready")
            down_done, h_ready, up_done, x_ready, stored = s("down_done"), s("h_ready"), s("up_done"), s("x_ready"), s("stored")
            BACK, LOOP0 = 2, 3
            ROUNDS = (ITEMS - 1 - LOOP0) // RING
            NBEST, WHICH, MIXED, HOT_T, BIASD, BIASU_PARTS = 3, 7, 14, 16, 17, 22

            def steps(engine, emit):
                def peeled(n):
                    emit(n, n % RING, lambda k: 0 <= n + k < ITEMS)
                for n in range(-1, LOOP0):
                    peeled(n)
                with engine.Fori(0, ROUNDS) as i:
                    for u in range(RING):
                        emit(i * RING + (LOOP0 + u), (LOOP0 + u) % RING, lambda k: True)
                for n in range(LOOP0 + ROUNDS * RING, ITEMS + BACK):
                    peeled(n)

            def experts_of_two(item, engine):
                return nc.values_load_multi_w_load_instructions(index[0:1, bass.ds(item * TOP, 2 * TOP)], engines=(engine.engine,),
                                                                min_val=0, max_val=EXPERTS - 1)[1]

            with nc.Block() as block:

                @block.gpsimd
                def _(pool):
                    pool.wait_ge(index_in, 16)
                    experts = [None]

                    def step(n, r, live):
                        if live(1):
                            if (r + 1) % 2 == 0:
                                experts[0] = experts_of_two(n + 1, pool)
                            if live(-3):
                                pool.wait_ge(down_done, (n - 3) + 1)
                            for k in range(TOP):
                                which_k = experts[0][(r + 1) % 2 * TOP + k]
                                last = nc.gpsimd.tensor_copy(wd[(r + 1) % RING][:, k:k + 1, :], down_sb[:, bass.ds(which_k, 1), :])
                            last.then_inc(wd_ready, 1)
                    steps(pool, step)

                @block.vector
                def _(dve):
                    count = [0]

                    def link(ins):
                        count[0] += 1
                        ins.then_inc(dve_g, 1)
                        dve.wait_ge(dve_g, count[0])

                    dve.wait_ge(pe_g, 1)
                    link(nc.vector.tensor_scalar(logit[:, :], banks[0][0:ITEMS, 0:EXPERTS], 1.0 / TOKENS, None, ALU.mult))
                    link(nc.vector.max(best[:, :], logit[:, :]))
                    link(nc.vector.tensor_scalar(nbest[:, :], best[:, 0:1], -1.0, None, ALU.mult))
                    dve.wait_ge(act_g, 1)
                    link(nc.vector.reciprocal(tsum[:, :], esum[:, :]))
                    link(nc.vector.tensor_scalar(gate[:, :], e[:, :], tsum[:, :], None, ALU.mult))
                    link(nc.vector.max(top[:, :], gate[:, :]))
                    link(nc.vector.max_index(which[:, :], top[:, :], gate[:, :]))
                    link(nc.vector.tensor_copy(whichf[:, :], which[:, 0:TOP]))
                    link(nc.vector.tensor_scalar(tsum[:, :], top[:, 0:1], top[:, 1:2], 1e-8, ALU.add, ALU.add))
                    link(nc.vector.reciprocal(tsum[:, :], tsum[:, :]))
                    link(nc.vector.tensor_scalar(wt[:, :], top[:, 0:TOP], tsum[:, :], None, ALU.mult))
                    for k in range(TOP):
                        nc.vector.tensor_copy(wide[:, k, :], wt[:, k:k + 1].broadcast_to([ITEMS, HIDDEN]))
                        last = nc.vector.tensor_scalar(hot[:, k, :], iota_sb[:, :], whichf[:, k:k + 1], None, ALU.is_equal)
                    link(last)
                    link(nc.vector.tensor_scalar(mix[:, :], hot[:, 0, :], wt[:, 0:1], None, ALU.mult))
                    link(nc.vector.scalar_tensor_tensor(out=mix[:, :], in0=hot[:, 1, :], scalar=wt[:, 1:2], in1=mix[:, :],
                                                        op0=ALU.mult, op1=ALU.add))
                    dve.wait_ge(pe_g, 2)
                    link(nc.vector.tensor_copy(weight[:, :], banks[1][:, 0:ITEMS]))
                    link(nc.vector.tensor_copy(hotT[:, :, :].rearrange("p a b -> p (a b)"), banks[2][0:EXPERTS, 0:(TOP + 3) * ITEMS]))
                    dve.wait_ge(pe_g, 3)
                    link(nc.vector.tensor_copy(biasd[:, :], banks[3][:, 0:ITEMS]))
                    link(nc.vector.tensor_copy(biasu[:, :], banks[4][0:3 * ITEMS, 0:WIDTH]))
                    link(nc.vector.tensor_copy(biasu_parts[:, :], biasu[:, :]))
                    link(nc.vector.tensor_tensor(biasu_rest[:, :], biasu[:, :], biasu_parts[:, :], ALU.subtract))
                    link(nc.vector.tensor_copy(biasu_mid[:, :], biasu_rest[:, :]))
                    mid_rows, lo_rows = slice(ITEMS, 2 * ITEMS), slice(2 * ITEMS, 3 * ITEMS)
                    nc.vector.tensor_copy(biasu_parts[mid_rows, :], biasu_mid[mid_rows, :])
                    link(nc.vector.tensor_tensor(biasu_parts[lo_rows, :], biasu_rest[lo_rows, :], biasu_mid[lo_rows, :], ALU.subtract))
                    assert count[0] == BIASU_PARTS

                    dve.wait_ge(index_in, 16)
                    experts = [None]

                    def step(n, r, live):
                        if live(1):
                            if (r + 1) % 2 == 0:
                                experts[0] = experts_of_two(n + 1, dve)
                            if live(-3):
                                dve.wait_ge(up_done, (n - 3) + 1)
                            for k in range(TOP):
                                half = slice(HIDDEN * k, HIDDEN * (k + 1))
                                which_k = experts[0][(r + 1) % 2 * TOP + k]
                                last = nc.vector.tensor_scalar(wu[(r + 1) % RING][half, :].unsqueeze(1), up_sb[half, bass.ds(which_k, 1), :],
                                                               weight[half, bass.ds(n + 1, 1)], None, ALU.mult)
                            last.then_inc(wu_ready, 1)
                        if live(-2):
                            dve.wait_ge(up_done, (n - 2) + 1)
                            xs = x[:, bass.ds((n - 2) * TILES, TILES), :]
                            src = o_bank[r % 2][:, 0:TOKENS].rearrange("p (t d) -> p t d", t=TILES)
                            nc.vector.tensor_tensor(xs, xs, src, ALU.add).then_inc(x_ready, 1)
                    steps(dve, step)

                @block.scalar
                def _(act):
                    act.wait_ge(dve_g, NBEST)
                    nc.scalar.activation(e[:, :], logit[:, :], ACT.Exp, bias=nbest[:, :], accum_out=esum[:, :]).then_inc(act_g, 1)
                    nc.scalar.preload_act_table(ACT.Gelu)
                    act.wait_ge(dve_g, BIASD)

                    def step(n, r, live):
                        if live(0):
                            act.wait_ge(down_done, n + 1)
                            if live(-2):
                                act.wait_ge(up_done, (n - 2) + 1)
                            nc.scalar.activation(hT[r % 2][:, :], t_bank[r % 2][:, 0:TOKENS], ACT.Gelu,
                                                 bias=biasd[:, bass.ds(n, 1)]).then_inc(h_ready, 1)
                    steps(act, step)

                @block.tensor
                def _(pe):
                    nc.tensor.matmul(banks[0][0:ITEMS, 0:EXPERTS], pooled[:, :], gate_sb[:, :], start=True, stop=True).then_inc(pe_g, 1)
                    pe.wait_ge(dve_g, MIXED)
                    nc.tensor.transpose(banks[1][:, 0:ITEMS], wide[:, :, :].rearrange("p a b -> p (a b)"), ident[0:ITEMS, 0:ITEMS])
                    for k in range(TOP + 3):
                        src = hot[:, k, :] if k < TOP else mix[:, :]
                        last = nc.tensor.transpose(banks[2][0:EXPERTS, k * ITEMS:(k + 1) * ITEMS], src, ident[0:ITEMS, 0:ITEMS])
                    last.then_inc(pe_g, 1)
                    pe.wait_ge(dve_g, HOT_T)
                    for k in range(TOP):
                        nc.tensor.matmul(banks[3][HIDDEN * k:HIDDEN * (k + 1), 0:ITEMS], downb_sb[:, :], hotT[:, k, :], start=True, stop=True)
                    nc.tensor.matmul(banks[4][0:3 * ITEMS, 0:WIDTH], hotT[:, TOP:, :].rearrange("p a b -> p (a b)"), upb_sb[:, :],
                                     start=True, stop=True).then_inc(pe_g, 1)
                    pe.wait_ge(dve_g, BIASU_PARTS)

                    def step(n, r, live):
                        if live(0):
                            pe.wait_ge(wd_ready, n + 1)
                            if live(-2):
                                pe.wait_ge(h_ready, (n - 2) + 1)
                            nc.tensor.matmul(t_bank[r % 2][:, 0:TOKENS], wd[r][:, :, :].rearrange("p a b -> p (a b)"),
                                             normT[:, bass.ds(n, 1), :], start=True, stop=True).then_inc(down_done, 1)
                        if live(-2):
                            z = (r - 2) % RING
                            if live(-4):
                                pe.wait_ge(x_ready, (n - 4) + 1)
                            acc = o_bank[r % 2]
                            nc.tensor.matmul(acc[:, 0:TOKENS].rearrange("p (t d) -> p t d", t=TILES),
                                             pick[:, bass.ds(n - 2, 1)].broadcast_to([3 * ITEMS, P]),
                                             biasu_parts[:, :].unsqueeze(1).broadcast_to([3 * ITEMS, TILES, WIDTH]),
                                             start=True, stop=False, skip_group_check=True)
                            pe.wait_ge(wu_ready, (n - 2) + 1)
                            pe.wait_ge(h_ready, (n - 2) + 1)
                            for t in range(TILES):
                                last = nc.tensor.matmul(acc[:, t * P:(t + 1) * P], hT[r % 2][:, t * P:(t + 1) * P], wu[z][:, :],
                                                        start=False, stop=(t == TILES - 1), skip_group_check=True)
                            last.then_inc(up_done, 1)
                    steps(pe, step)

                @block.sync
                def _(sp):
                    sp.wait_ge(dve_g, WHICH)
                    sp.dma_start(index[0:1, :].rearrange("a (n k) -> a n k", k=TOP), which[:, 0:TOP]).then_inc(index_in, 16)
                    sp.wait_ge(index_in, 16)
                    if not store:
                        constant_rows(sp, 1)
                        sp.wait_ge(tail_in, 2 * 16 * 16)
                    if store:
                        def step(n, r, live):
                            if live(-2):
                                sp.wait_ge(x_ready, (n - 2) + 1)
                                at = bass.ds((n - 2) * TILES, TILES)
                                sp.dma_start(out_dram[:, at, :], x[:, at, :]).then_inc(stored, 16)
                        steps(sp, step)
                        sp.wait_ge(stored, 16 * ITEMS)

        attention("a", wa, True, float(HEAD) ** -0.5, True)
        feed_forward("fa", False)
        attention("b", wb, False, float(WIDTH) ** -0.5, False)
        feed_forward("fb", True)


def kernel(L0_attn_a_x, L0_attn_a_Wq, L0_attn_a_bq, L0_attn_a_Wk, L0_attn_a_bk, L0_attn_a_Wv, L0_attn_a_bv, L0_attn_a_Wo,
           L0_attn_b_w_qkv, L0_attn_b_w_out, L0_ffn_gate_w, L0_ffn_down_w, L0_ffn_down_b, L0_ffn_up_w, L0_ffn_up_b):
    import ml_dtypes
    import concourse.bacc as bacc
    from concourse.bass_utils import run_bass_kernel_spmd

    def heads_last(m):
        m = np.asarray(m)
        return m.reshape(m.shape[0], PAIRS, 2, HEAD).transpose(0, 2, 3, 1).reshape(m.shape[0], WIDTH)

    def shared(m):
        m = np.asarray(m)
        return m.reshape(SHARES, IN_SHARE, PER_GROUP, HEAD, -1).transpose(0, 2, 1, 3, 4).reshape(m.shape)

    t = lambda m: np.asarray(m).T
    col = lambda v: np.asarray(v).reshape(1, WIDTH)
    w_qkv = np.asarray(L0_attn_b_w_qkv)
    arrays = {
        "x": np.asarray(L0_attn_a_x),
        "attn_a": np.concatenate([heads_last(t(L0_attn_a_Wq)), heads_last(t(L0_attn_a_Wk)), t(L0_attn_a_Wv), shared(t(L0_attn_a_Wo)),
                                  heads_last(col(L0_attn_a_bq)).T, heads_last(col(L0_attn_a_bk)).T, shared(col(L0_attn_a_bv).T)], 1),
        "attn_b": np.concatenate([heads_last(w_qkv[:, 0:128]), heads_last(w_qkv[:, 128:256]), w_qkv[:, 256:384],
                                  shared(L0_attn_b_w_out)], 1),
        "gate_w": t(L0_ffn_gate_w),
        "down_w": np.asarray(L0_ffn_down_w).transpose(2, 0, 1),
        "down_b": np.asarray(L0_ffn_down_b),
        "up_w": np.asarray(L0_ffn_up_w).transpose(2, 0, 1),
        "up_b": np.asarray(L0_ffn_up_b),
        "tail": rows_of_constants().astype(ml_dtypes.bfloat16),
        "ident": np.eye(P, dtype=np.float32),
        "iota": np.tile(np.arange(EXPERTS, dtype=np.float32), (ITEMS, 1)),
        "pick": np.tile(np.eye(ITEMS), (3, 1)).astype(ml_dtypes.bfloat16),
    }
    arrays = {f"in_{k}": np.ascontiguousarray(v) for k, v in arrays.items()}
    nc = bacc.Bacc("TRN2", target_bir_lowering=False, num_devices=1)
    args = [nc.dram_tensor(k, v.shape, mybir.dt.from_np(v.dtype), kind="ExternalInput").ap() for k, v in arrays.items()]
    out = nc.dram_tensor("out", (ITEMS, TOKENS, WIDTH), FP32, kind="ExternalOutput").ap()
    build(nc, *args, out)
    r = run_bass_kernel_spmd(nc, [arrays], core_ids=[0])
    return r.results[0]["out"]
```

```python
import numpy as np

import concourse.bass as bass
from concourse import mybir
from contextlib import ExitStack

FP32 = mybir.dt.float32
BF16 = mybir.dt.bfloat16
U32 = mybir.dt.uint32
ALU = mybir.AluOpType
ACT = mybir.ActivationFunctionType
AX = mybir.AxisListType

P = 128
ITEMS, TOKENS, WIDTH = 32, 256, 128
TILES = TOKENS // P
HEADS, HEAD = 16, 8
PAIRS = HEADS // 2
EXPERTS, HIDDEN, TOP = 8, 64, 2
EPS = 1e-5
NEG = -1.0e30

Q_PARTS = (0, 0, 0, 1, 1, 2)
K_PARTS = (0, 1, 2, 0, 1, 0)
SLOTS = len(Q_PARTS)
BLOCK = 64
MASK_ROW = SLOTS * HEAD
MAX_ROW = MASK_ROW + 2
ALL_SLOTS = BLOCK // HEAD

CONSTANTS = 11
CHUNKS = ((0, 2), (2, 9), (9, ITEMS))
RING = 4
GROUPS, PER_GROUP = 4, 4
SHARES, IN_SHARE = 2, 2
SUMS = HEAD + 1


def rows_of_constants():
    tail = np.zeros((2, BLOCK - MASK_ROW, 2, TOKENS), np.float32)
    tail[0, 0, 0, 0] = NEG
    tail[0, 1, 0, TOKENS - 1] = NEG
    tail[:, 0, 1, TOKENS - 1] = 1.0
    tail[:, 1, 1, 0] = 1.0
    tail[:, 2:5, 1, :] = 1.0
    tail = tail.transpose(0, 2, 1, 3).reshape(2, 2, ALL_SLOTS - SLOTS, 1, HEAD, 1, TOKENS)
    return np.broadcast_to(tail, (2, 2, ALL_SLOTS - SLOTS, 2, HEAD, PAIRS, TOKENS)).reshape(2, 2, ALL_SLOTS - SLOTS, P, TOKENS)


def build(nc, x_dram_in, attn_w, attn_b, gate_w, down_w, down_b, up_w, up_b, tail_c, ident_c, iota_c, pick_c, out):
    ctx = ExitStack()
    with ctx:
        def sb(name, shape, dt=FP32):
            return ctx.enter_context(nc.sbuf_tensor(name, shape, dt))

        def sem(name):
            return ctx.enter_context(nc.semaphore(name))

        x = sb("x", [P, ITEMS * TILES, WIDTH])
        normT = sb("normT", [P, ITEMS, TOKENS])
        pooled = sb("pooled", [P, ITEMS])
        q_stack = [sb(f"q_stack{r}", [P, PAIRS, TOKENS], BF16) for r in range(RING)]
        k_stack = [sb(f"k_stack{r}", [P, PAIRS, 2, TOKENS], BF16) for r in range(RING)]
        values = [sb(f"values{r}", [P, TILES, HEADS, 32]) for r in range(RING)]
        qk32 = [sb(f"qk32_{i}", [P, 2, TOKENS]) for i in range(2)]
        rest = [sb(f"rest{i}", [P, 2, TOKENS]) for i in range(2)]
        parts = [sb(f"parts{i}", [P, 3, 2, TOKENS], BF16) for i in range(2)]
        probs = [sb(f"probs{i}", [P, PER_GROUP, TILES, TOKENS]) for i in range(2)]
        xn = [sb(f"xn{i}", [P, TILES, WIDTH]) for i in range(2)]
        yn = [sb(f"yn{i}", [P, TILES, WIDTH]) for i in range(2)]
        xnT = [sb(f"xnT{i}", [P, TOKENS]) for i in range(2)]
        raw = [sb(f"raw{i}", [P, TILES, 6]) for i in range(4)]
        mv = [sb(f"mv{i}", [P, TILES, 2]) for i in range(4)]
        varp = [sb(f"varp{i}", [P, TILES]) for i in range(4)]
        rstd = [sb(f"rstd{i}", [P, TILES]) for i in range(4)]
        nmax = [sb(f"nmax{i}", [P, TILES, HEADS]) for i in range(2)]
        mrest = [sb(f"mrest{i}", [P, TILES * HEADS]) for i in range(2)]
        mparts = [sb(f"mparts{i}", [P, TILES * 2, 3, PAIRS], BF16) for i in range(2)]
        maxT = [sb(f"maxT{i}", [2 * 3 * PAIRS, TOKENS], BF16) for i in range(2)]
        oT = [sb(f"oT{i}", [P, SHARES, TOKENS]) for i in range(2)]
        rsum = sb("rsum", [P, TILES * HEADS // IN_SHARE, IN_SHARE])
        o = sb("o", [P, TILES, WIDTH])
        onT = sb("onT", [P, TOKENS])
        wa = sb("wa", [P, 4 * WIDTH + 3])
        wb = sb("wb", [P, 4 * WIDTH])
        bqs = sb("bqs", [P, 1])
        ident = sb("ident", [P, P])
        identb = sb("identb", [P, P], BF16)
        minus_half = sb("minus_half", [P, TILES])
        gate_sb = sb("gate_sb", [P, EXPERTS])
        down_sb = sb("down_sb", [P, EXPERTS, HIDDEN])
        up_sb = sb("up_sb", [P, EXPERTS, WIDTH])
        downb_sb = sb("downb_sb", [EXPERTS, HIDDEN])
        upb_sb = sb("upb_sb", [EXPERTS, WIDTH])
        iota_sb = sb("iota_sb", [ITEMS, EXPERTS])

        logit = sb("logit", [ITEMS, EXPERTS])
        best = sb("best", [ITEMS, 8])
        nbest = sb("nbest", [ITEMS, 1])
        e = sb("e", [ITEMS, EXPERTS])
        esum = sb("esum", [ITEMS, 1])
        gate = sb("gate", [ITEMS, EXPERTS])
        top = sb("top", [ITEMS, 8])
        which = sb("which", [ITEMS, 8], U32)
        whichf = sb("whichf", [ITEMS, TOP])
        tsum = sb("tsum", [ITEMS, 1])
        wt = sb("wt", [ITEMS, TOP])
        wide = sb("wide", [ITEMS, TOP, HIDDEN])
        hot = sb("hot", [ITEMS, TOP, EXPERTS])
        mix = sb("mix", [ITEMS, EXPERTS])
        weight = sb("weight", [P, ITEMS])
        hotT = sb("hotT", [EXPERTS, TOP + 3, ITEMS])
        biasd = sb("biasd", [P, ITEMS])
        biasu = sb("biasu", [3 * ITEMS, WIDTH])
        biasu_rest = sb("biasu_rest", [3 * ITEMS, WIDTH])
        biasu_mid = sb("biasu_mid", [3 * ITEMS, WIDTH], BF16)
        biasu_parts = sb("biasu_parts", [3 * ITEMS, WIDTH], BF16)
        pick = sb("pick", [3 * ITEMS, ITEMS], BF16)
        index = sb("index", [1, ITEMS * TOP], U32)
        wd = [sb(f"wd{i}", [P, TOP, HIDDEN]) for i in range(RING)]
        wu = [sb(f"wu{i}", [P, WIDTH]) for i in range(RING)]
        hT = [sb(f"hT{i}", [P, TOKENS]) for i in range(2)]

        scratch = {m: [nc.dram_tensor(f"scratch{m}{i}", [2 * ALL_SLOTS, P, TOKENS], BF16, kind="Internal").ap() for i in range(2)]
                   for m in range(2)}
        tail_in = sem("tail_in")

        def constant_rows(sp, m):
            for D in scratch[m]:
                for qk in range(2):
                    dst = D[ALL_SLOTS * qk + SLOTS:ALL_SLOTS * (qk + 1)]
                    sp.dma_start(dst, tail_c[m, qk]).then_inc(tail_in, 16)

        def of_group(r, g):
            return values[r][:, :, :, :].rearrange("p t (b c) w -> p (t b) c w", c=PER_GROUP)[:, g::IN_SHARE]

        banks = [ctx.enter_context(nc.psum_tensor(f"bank{i}", [P, 512], FP32)) for i in range(8)]
        s_bank, t_bank, o_bank, m_bank = banks[0:2], banks[2:4], banks[4:6], banks[6:8]

        x_dram = x_dram_in.rearrange("b (t p) d -> p (b t) d", p=P)
        out_dram = out.rearrange("b (t p) d -> p (b t) d", p=P)

        apart = {}

        def wait_apart(engine, signal, value):
            if not isinstance(value, int):
                if engine.engine not in apart:
                    apart[engine.engine] = engine.alloc_register("apart")
                register = apart[engine.engine]
                engine.reg_mov(register, value)
                value = engine.snap(register)
            engine.wait_ge(consts_in, 16)
            engine.wait_ge(signal, value)

        consts_in = sem("consts_in")
        x_in = [sem(f"x_in{c}") for c in range(len(CHUNKS))]
        set_up = sem("set_up")
        with nc.Block() as block:

            @block.sync
            def _(sp):
                for c, (first, end) in enumerate(CHUNKS):
                    at = slice(first * TILES, end * TILES)
                    sp.dma_start(x[:, at, :], x_dram[:, at, :]).then_inc(x_in[c], 16)
                    if c == 0:
                        constant_rows(sp, 0)
                    if c == 1:
                        sp.wait_ge(consts_in, 16 * CONSTANTS)

            @block.scalar
            def _(act):
                loads = [(wa[:, :], attn_w[:, :]), (ident[:, :], ident_c[:, :]), (wb[:, :], attn_b[:, :]), (gate_sb[:, :], gate_w[:, :]),
                         (down_sb[:, :, :], down_w[:, :, :]), (upb_sb[:, :], up_b[:, :]), (downb_sb[:, :], down_b[:, :]),
                         (iota_sb[:, :], iota_c[:, :]), (pick[:, :], pick_c[:, :])]
                loads += [(up_sb[HIDDEN * k:HIDDEN * (k + 1), :, :], up_w[:, :, :]) for k in range(TOP)]
                assert len(loads) == CONSTANTS
                for dst, src in loads:
                    act.dma_start(dst, src).then_inc(consts_in, 16)
                act.wait_ge(consts_in, 16 * len(loads))
                nc.scalar.mul(bqs[:, :], wa[:, 512:513], float(HEAD) ** -0.5)
                nc.scalar.copy(identb[:, :], ident[:, :])

            @block.gpsimd
            def _(pool):
                nc.gpsimd.memset(minus_half[:, :], -0.5)
                for r in range(RING):
                    nc.gpsimd.memset(values[r][:, :, :, :], 0.0).then_inc(set_up, 1)
                for r in range(RING):
                    pool.wait_ge(set_up, r + 1)
                    for g in range(IN_SHARE):
                        at = SUMS * g + HEAD
                        nc.gpsimd.memset(of_group(r, g)[:, :, :, at:at + 1], 1.0)

            @block.vector
            def _(dve):
                for r in range(RING):
                    for par in range(2):
                        others = k_stack[r][BLOCK * (1 - par):BLOCK * (2 - par), :, par, :]
                        nc.vector.memset(others.bitcast(FP32), 0.0)

        def attention(name, w, bias, scale, masked):
            BACK, AHEAD, LOOP0 = 2, 5, 4
            ROUNDS = (ITEMS - AHEAD - LOOP0) // RING
            LOOP1 = LOOP0 + ROUNDS * RING

            def s(what):
                return sem(f"{name}_{what}")

            raw_done, mv_done = s("raw_done"), s("mv_done")
            var_done, rstd_done, xn_ready = s("var_done"), s("rstd_done"), s("xn_ready")
            xT_done, xnT_ready = s("xT_done"), s("xnT_ready")
            qk_done, qk32_ready, hi_ready = s("qk_done"), s("qk32_ready"), s("hi_ready")
            v_done, v_ready = s("v_done"), s("v_ready")
            rest_done, mid_done, parts_ready = s("rest_done"), s("mid_done"), s("parts_ready")
            bounced = [s(f"bounced{i}") for i in range(2)]
            stack_in = [s(f"stack_in{i}") for i in range(2)]
            s_done, max_done = s("s_done"), s("max_done")
            mhi_done, mrest_done, mmid_done, mparts_ready = s("mhi_done"), s("mrest_done"), s("mmid_done"), s("mparts_ready")
            mT_done, maxT_ready = s("mT_done"), s("maxT_ready")
            max_in = [s(f"max_in{i}") for i in range(2)]
            t_done, exp_done = s("t_done"), s("exp_done")
            pv_done = s("pv_done")
            oT_ready = s("oT_ready")
            on_done, rsum_done, o_ready = s("on_done"), s("rsum_done"), s("o_ready")
            oT2_done, onT_ready = s("oT2_done"), s("onT_ready")
            wo_done, x_ready = s("wo_done"), s("x_ready")
            raw2, mv2, var2, rstd2, yn_ready = s("raw2"), s("mv2"), s("var2"), s("rstd2"), s("yn_ready")
            yT_done, yT_ready = s("yT_done"), s("yT_ready")

            wq, wk, wv, wo = (w[:, i * WIDTH:(i + 1) * WIDTH] for i in range(4))

            def one_step(emit, n):
                emit(n, n % RING, lambda k: 0 <= n + k < ITEMS, lambda k: (n + k) // 2)

            def steps(engine, emit, first):
                for n in range(first, LOOP0):
                    one_step(emit, n)
                with engine.Fori(0, ROUNDS) as i:
                    for u in range(RING):
                        emit(i * RING + (LOOP0 + u), (LOOP0 + u) % RING, lambda k: True,
                             lambda k: i * (RING // 2) + (LOOP0 + u + k) // 2)
                for n in range(LOOP1, ITEMS + BACK):
                    one_step(emit, n)

            def tiles_of(item):
                return bass.ds(item * TILES, TILES)

            def tile_of(item, t):
                return bass.ds(item * TILES + t, 1)


            def sync_program(sp):
                sp.wait_ge(tail_in, 4 * 16 if masked else 2 * 4 * 16)

                def step(n, r, live, half):
                    if live(3):
                        D = scratch[0 if masked else 1][(r + 3) % 2]
                        sp.wait_ge(bounced[(r + 3) % 2], half(3) * 96 + 96)
                        if live(-1):
                            sp.wait_ge(t_done, (n - 1) * HEADS + HEADS)
                        for par in range(2):
                            rows = slice(BLOCK * par, BLOCK * (par + 1))
                            q_src, k_src = (D[ALL_SLOTS * qk:ALL_SLOTS * (qk + 1)].rearrange("s (x d j) t -> s x d (j t)", x=2, d=HEAD)[:, par]
                                            for qk in range(2))
                            sp.dma_start(q_stack[(r + 3) % RING][rows, :, :].rearrange("p j t -> p (j t)"),
                                         q_src).then_inc(stack_in[(r + 3) % 2], 16)
                            sp.dma_start(k_stack[(r + 3) % RING][rows, :, par, :], k_src).then_inc(stack_in[(r + 3) % 2], 16)
                    if live(1):
                        sp.wait_ge(maxT_ready, (n + 1) + 1)
                        for par in range(2):
                            dst = q_stack[(r + 1) % RING][BLOCK * par + MAX_ROW:BLOCK * par + MAX_ROW + 3, :, :]
                            sp.dma_start(dst, maxT[(r + 1) % 2][3 * PAIRS * par:3 * PAIRS * (par + 1), :]).then_inc(max_in[(r + 1) % 2], 16)
                    if live(4):
                        D, i = scratch[0 if masked else 1][(r + 4) % 2], (r + 4) % 2
                        sp.wait_ge(parts_ready, (n + 4) + 1)
                        if live(2):
                            sp.wait_ge(stack_in[(r + 2) % 2], half(2) * 64 + 64)
                        at = 0
                        for part in range(3):
                            count = Q_PARTS.count(part)
                            q_src = parts[i][:, part, 0].unsqueeze(1).broadcast_to([P, count, TOKENS])
                            sp.dma_start(D[at:at + count].rearrange("s p t -> p s t"), q_src).then_inc(bounced[(r + 4) % 2], 16)
                            k_src = parts[i][:, 0:count, 1]
                            sp.dma_start(D[ALL_SLOTS + at:ALL_SLOTS + at + count].rearrange("s p t -> p s t"), k_src).then_inc(bounced[(r + 4) % 2], 16)
                            at += count
                return step

            def gpsimd_program(pool):
                def split(src, tmp, hi, mid, lo, hi_done, rest_d, mid_d, lo_d, item):
                    pool.wait_ge(hi_done, item + 1)
                    nc.gpsimd.tensor_tensor(tmp, src, hi, ALU.subtract).then_inc(rest_d, 1)
                    wait_apart(pool, rest_d, item + 1)
                    nc.gpsimd.tensor_scalar(mid, tmp, 1.0, 0.0, ALU.mult, ALU.add).then_inc(mid_d, 1)
                    pool.wait_ge(mid_d, item + 1)
                    nc.gpsimd.tensor_tensor(lo, tmp, mid, ALU.subtract).then_inc(lo_d, 1)

                def inverse_deviation(item, i, mv_d, var_d, rstd_d):
                    wait_apart(pool, mv_d, item + 1)
                    nc.gpsimd.tensor_scalar(varp[i][:, :], mv[i][:, :, 1], 1.0, EPS, ALU.mult, ALU.add).then_inc(var_d, 1)
                    pool.wait_ge(var_d, item + 1)
                    nc.gpsimd.tensor_tensor(rstd[i][:, :], varp[i][:, :], minus_half[:, :], ALU.pow).then_inc(rstd_d, 1)

                def step(n, r, live, half):
                    if live(1):
                        i = (r + 1) % 2
                        if live(-1):
                            pool.wait_ge(mT_done, (n - 1) + 1)
                        wait_apart(pool, max_done, (n + 1) * HEADS + HEADS)
                        src = nmax[i][:, :, :].rearrange("p t (x j) -> p (t x) j", x=2)
                        tmp = mrest[i][:, :].rearrange("p (a j) -> p a j", j=PAIRS)
                        nc.gpsimd.tensor_scalar(mparts[i][:, :, 0, :], src, 1.0, 0.0, ALU.mult, ALU.add).then_inc(mhi_done, 1)
                        split(src, tmp, mparts[i][:, :, 0, :], mparts[i][:, :, 1, :], mparts[i][:, :, 2, :],
                              mhi_done, mrest_done, mmid_done, mparts_ready, n + 1)
                    if live(5):
                        inverse_deviation(n + 5, (r + 5) % 2, mv_done, var_done, rstd_done)
                    if live(-2):
                        inverse_deviation(n - 2, 2 + r % 2, mv2, var2, rstd2)
                    if live(4):
                        i = (r + 4) % 2
                        pool.wait_ge(qk32_ready, (n + 4) + 1)
                        split(qk32[i][:, :, :], rest[i][:, :, :], parts[i][:, 0], parts[i][:, 1], parts[i][:, 2],
                              hi_ready, rest_done, mid_done, parts_ready, n + 4)
                return step

            def vector_program(dve):
                def stats(item, i, raw_d, mv_d):
                    for t in range(TILES):
                        last = nc.vector.bn_stats(raw[i][:, t, :], x[:, tile_of(item, t), :])
                    last.then_inc(raw_d, 1)

                def aggregate(item, i, raw_d, mv_d):
                    wait_apart(dve, raw_d, item + 1)
                    for t in range(TILES):
                        last = nc.vector.bn_aggr(mv[i][:, t, :], raw[i][:, t, :])
                    last.then_inc(mv_d, 1)

                def normalise(item, i, dst, rstd_d, dst_d):
                    dve.wait_ge(rstd_d, item + 1)
                    for t in range(TILES):
                        last = nc.vector.tensor_scalar(dst[:, t:t + 1, :], x[:, tile_of(item, t), :], mv[i][:, t, 0:1],
                                                       rstd[i][:, t:t + 1], ALU.subtract, ALU.mult)
                    last.then_inc(dst_d, 1)

                def step(n, r, live, half):
                    for p in range(PAIRS):
                        if live(2):
                            i = (r + 2) % 2
                            if p == 0 and live(0):
                                dve.wait_ge(mparts_ready, n + 1)
                            for t in range(TILES):
                                dve.wait_ge(s_done, (n + 2) * HEADS + (2 * p + t + 1))
                                src = s_bank[t][:, :].rearrange("p (x k) -> p x k", x=2)
                                dst = nmax[i][:, t, :].rearrange("p (x j) -> p x j", x=2)[:, :, p:p + 1]
                                nc.vector.tensor_reduce(dst, src, axis=AX.X, op=ALU.max, negate=True).then_inc(max_done, 1)
                        if p == 0 and live(-2):
                            dve.wait_ge(wo_done, (n - 2) + 1)
                            xs = x[:, tiles_of(n - 2), :]
                            nc.vector.tensor_tensor(xs, xs, m_bank[1][:, 0:TOKENS].rearrange("p (t d) -> p t d", t=TILES),
                                                    ALU.add).then_inc(x_ready, 1)
                        if p == 0 and live(5):
                            for c, (start, _) in enumerate(CHUNKS):
                                if masked and isinstance(n, int) and n + 5 == start:
                                    wait_apart(dve, x_in[c], 16)
                            stats(n + 5, (r + 5) % 2, raw_done, mv_done)
                        if p == 1 and live(5):
                            if masked and isinstance(n, int) and n + 1 == LOOP0:
                                wait_apart(dve, x_in[-1], 16)
                            aggregate(n + 5, (r + 5) % 2, raw_done, mv_done)
                        if p == 5 and live(5):
                            if live(3):
                                dve.wait_ge(xT_done, (n + 3) + 1)
                            normalise(n + 5, (r + 5) % 2, xn[(r + 5) % 2], rstd_done, xn_ready)
                        if p == 3 and live(-1):
                            dve.wait_ge(on_done, (n - 1) + 1)
                            if live(-2):
                                dve.wait_ge(oT2_done, (n - 2) + 1)
                            both = m_bank[1][:, :].rearrange("p (m w) -> p m w", w=32)[:, :, 0:IN_SHARE * SUMS]
                            both = both.rearrange("p m (g e) -> p m g e", g=IN_SHARE)
                            nc.vector.reciprocal(rsum[:, :, :], both[:, :, :, HEAD]).then_inc(rsum_done, 1)
                            dve.wait_ge(rsum_done, (n - 1) + 1)
                            nc.vector.tensor_tensor(o[:, :, :].rearrange("p t (m g d) -> p (t m) g d", g=IN_SHARE, d=HEAD),
                                                    both[:, :, :, 0:HEAD], rsum[:, :, :].unsqueeze(3).broadcast_to(
                                                        [P, TILES * HEADS // IN_SHARE, IN_SHARE, HEAD]), ALU.mult).then_inc(o_ready, 1)
                        if p == 2 and live(-2):
                            wait_apart(dve, x_ready, (n - 2) + 1)
                            stats(n - 2, 2 + r % 2, raw2, mv2)
                        if p == 3 and live(-2):
                            aggregate(n - 2, 2 + r % 2, raw2, mv2)
                        if p == 5 and live(-2):
                            if live(-4):
                                dve.wait_ge(yT_done, (n - 4) + 1)
                            normalise(n - 2, 2 + r % 2, yn[r % 2], rstd2, yn_ready)
                return step

            def scalar_program(act):
                def step(n, r, live, half):
                    for p in range(PAIRS):
                        if live(0):
                            for h in (2 * p, 2 * p + 1):
                                g, c = divmod(h, PER_GROUP)
                                if c == 0 and g >= 2:
                                    act.wait_ge(pv_done, n * GROUPS + (g - 1))
                                elif c == 0 and live(-1):
                                    act.wait_ge(pv_done, (n - 1) * GROUPS + (g + 3))
                                act.wait_ge(t_done, n * HEADS + (h + 1))
                                nc.scalar.activation(probs[g % 2][:, c, :, :], t_bank[h % 2][:, :].rearrange("p (k q) -> p k q", k=TILES),
                                                     ACT.Exp).then_inc(exp_done, 1)

                        def values_out(item, i, a):
                            act.wait_ge(pv_done, item * GROUPS + IN_SHARE * (a + 1))
                            nc.scalar.copy(oT[i][:, a, :], o_bank[a][:, 0:TOKENS]).then_inc(oT_ready, 1)

                        if p == 0 and live(4):
                            act.wait_ge(xT_done, (n + 4) + 1)
                            nc.scalar.copy(xnT[(r + 4) % 2][:, :], m_bank[0][:, 0:TOKENS]).then_inc(xnT_ready, 1)
                        if p == 1 and live(-1):
                            values_out(n - 1, (r - 1) % 2, 1)
                        if p == 1 and live(1):
                            act.wait_ge(mT_done, (n + 1) + 1)
                            if live(-1):
                                act.wait_ge(max_in[(r - 1) % 2], half(-1) * 32 + 32)
                            nc.scalar.copy(maxT[(r + 1) % 2][:, :],
                                           m_bank[1][:, :].bitcast(BF16)[0:6 * PAIRS, 0:TOKENS]).then_inc(maxT_ready, 1)
                        if p in (2, 3) and live(4):
                            i = (r + 4) % 2
                            if p == 2:
                                act.wait_ge(qk_done, (n + 4) + 1)
                                if live(2):
                                    act.wait_ge(parts_ready, (n + 2) + 1)
                                    act.wait_ge(bounced[(r + 2) % 2], half(2) * 96 + 96)
                            src = m_bank[0][:, :].rearrange("p (a t) -> p a t", a=2)
                            dst, signal = ((qk32[i], qk32_ready), (parts[i][:, 0], hi_ready))[p - 2]
                            if bias:
                                nc.scalar.activation(dst[:, 0, :], src[:, 0, :], ACT.Identity, bias=bqs[:, :], scale=scale)
                                last = nc.scalar.activation(dst[:, 1, :], src[:, 1, :], ACT.Identity, bias=w[:, 513:514])
                            else:
                                nc.scalar.mul(dst[:, 0, :], src[:, 0, :], scale)
                                last = nc.scalar.copy(dst[:, 1, :], src[:, 1, :])
                            last.then_inc(signal, 1)
                        if p == 5 and live(0):
                            values_out(n, r % 2, 0)
                        if p == 5 and live(3):
                            act.wait_ge(v_done, (n + 3) + 1)
                            if live(-1):
                                act.wait_ge(pv_done, (n - 1) * GROUPS + 4)
                            src = m_bank[0][:, 0:TOKENS].rearrange("p (b c d) -> p b c d", c=PER_GROUP, d=HEAD)
                            for g in range(IN_SHARE):
                                last = nc.scalar.copy(of_group((r + 3) % RING, g)[:, :, :, SUMS * g:SUMS * g + HEAD], src[:, g::IN_SHARE])
                            last.then_inc(v_ready, 1)
                        if p == 6 and live(-1):
                            act.wait_ge(oT2_done, (n - 1) + 1)
                            if live(-2):
                                act.wait_ge(wo_done, (n - 2) + 1)
                            if bias:
                                last = nc.scalar.activation(onT[:, :], m_bank[1][:, 0:TOKENS], ACT.Identity, bias=w[:, 514:515])
                            else:
                                last = nc.scalar.copy(onT[:, :], m_bank[1][:, 0:TOKENS])
                            last.then_inc(onT_ready, 1)
                        if p == 7 and live(-2):
                            act.wait_ge(yT_done, (n - 2) + 1)
                            nc.scalar.activation(normT[:, bass.ds(n - 2, 1), :], m_bank[0][:, 0:TOKENS].unsqueeze(1), ACT.Copy,
                                                 accum_out=pooled[:, bass.ds(n - 2, 1)]).then_inc(yT_ready, 1)
                return step

            def tensor_program(pe):
                def weigh(item, r, g):
                    pe.wait_ge(exp_done, item * HEADS + PER_GROUP * (g + 1))
                    a, g2 = divmod(g, IN_SHARE)
                    for k in range(TILES):
                        for c in range(PER_GROUP):
                            last = nc.tensor.matmul(o_bank[a][32 * c:32 * (c + 1), 0:TOKENS],
                                                    values[r % RING][:, k, PER_GROUP * g + c, :], probs[g % 2][:, c, k, :],
                                                    start=(g2 == 0 and k == 0), stop=(g2 == IN_SHARE - 1 and k == TILES - 1),
                                                    skip_group_check=True)
                    last.then_inc(pv_done, 1)

                def step(n, r, live, half):
                    for p in range(PAIRS):
                        z = (r + 2) % RING
                        if p == 0 and live(0):
                            pe.wait_ge(max_in[r % 2], half(0) * 32 + 32)
                        if p == 0 and live(2):
                            pe.wait_ge(stack_in[(r + 2) % 2], half(2) * 64 + 64)
                        for a in range(2):
                            h = 2 * p + a
                            if live(0):
                                if h >= 2:
                                    pe.wait_ge(exp_done, n * HEADS + (h - 1))
                                elif live(-1):
                                    pe.wait_ge(exp_done, (n - 1) * HEADS + (h + 15))
                                for k in range(TILES):
                                    last = nc.tensor.matmul(t_bank[a][:, k * TOKENS:(k + 1) * TOKENS],
                                                            k_stack[r][:, p, a, k * P:(k + 1) * P], q_stack[r][:, p, :],
                                                            start=(k == 0), stop=(k == TILES - 1))
                                last.then_inc(t_done, 1)
                            if live(2):
                                if h >= 2:
                                    pe.wait_ge(max_done, (n + 2) * HEADS + (h - 1))
                                elif live(1):
                                    pe.wait_ge(max_done, (n + 1) * HEADS + (h + 15))
                                nc.tensor.matmul(s_bank[a][:, :], q_stack[z][:, p, a * P:(a + 1) * P],
                                                 k_stack[z][:, p, :, :].rearrange("p x t -> p (x t)"),
                                                 start=True, stop=True).then_inc(s_done, 1)
                        if p == 0 and live(-1):
                            weigh(n - 1, r - 1, 3)
                        if p == 0 and live(4):
                            pe.wait_ge(xn_ready, (n + 4) + 1)
                            if live(-3):
                                pe.wait_ge(yT_ready, (n - 3) + 1)
                            elif live(2):
                                pe.wait_ge(v_ready, (n + 2) + 1)
                            elif live(3):
                                pe.wait_ge(hi_ready, (n + 3) + 1)
                            for t in range(TILES):
                                last = nc.tensor.transpose(m_bank[0][:, t * P:(t + 1) * P], xn[(r + 4) % 2][:, t, :], ident[:, :])
                            last.then_inc(xT_done, 1)
                        if p == 1 and live(1):
                            if live(-2):
                                pe.wait_ge(x_ready, (n - 2) + 1)
                            elif live(0):
                                pe.wait_ge(maxT_ready, n + 1)
                            wait_apart(pe, mparts_ready, (n + 1) + 1)
                            for t in range(TILES):
                                last = nc.tensor.transpose(m_bank[1][:, :].bitcast(BF16)[0:6 * PAIRS, t * P:(t + 1) * P],
                                                           mparts[(r + 1) % 2][:, 2 * t:2 * t + 2, :, :].rearrange("p a b j -> p (a b j)"),
                                                           identb[:, :])
                            last.then_inc(mT_done, 1)
                        if p == 1 and live(4):
                            pe.wait_ge(xnT_ready, (n + 4) + 1)
                            for a, wmat in enumerate((wq, wk)):
                                last = nc.tensor.matmul(m_bank[0][:, a * TOKENS:(a + 1) * TOKENS], wmat, xnT[(r + 4) % 2][:, :],
                                                        start=(a == 0), stop=(a == 1), skip_group_check=True)
                            last.then_inc(qk_done, 1)
                        if p == 2 and live(0):
                            if live(-1):
                                pe.wait_ge(oT_ready, (n - 1) * SHARES + 1)
                            weigh(n, r, 0)
                        if p == 3 and live(-1):
                            pe.wait_ge(oT_ready, (n - 1) * SHARES + 2)
                            if live(1):
                                pe.wait_ge(maxT_ready, (n + 1) + 1)
                            elif live(-2):
                                pe.wait_ge(x_ready, (n - 2) + 1)
                            for t in range(TILES):
                                for a in range(SHARES):
                                    at = (t * SHARES + a) * P
                                    last = nc.tensor.transpose(m_bank[1][:, at:at + P], oT[(r - 1) % 2][:, a, t * P:(t + 1) * P], ident[:, :])
                            last.then_inc(on_done, 1)
                        if p == 4 and live(0):
                            weigh(n, r, 1)
                        if p == 4 and live(3):
                            pe.wait_ge(xnT_ready, (n + 3) + 1)
                            if live(4):
                                pe.wait_ge(hi_ready, (n + 4) + 1)
                            elif live(-3):
                                pe.wait_ge(yT_ready, (n - 3) + 1)
                            for t in range(TILES):
                                last = nc.tensor.matmul(m_bank[0][:, t * P:(t + 1) * P], xnT[(r + 3) % 2][:, t * P:(t + 1) * P], wv,
                                                        start=(t == 0), stop=(t == TILES - 1), skip_group_check=True)
                            last.then_inc(v_done, 1)
                        if p == 5 and live(-1):
                            pe.wait_ge(o_ready, (n - 1) + 1)
                            for t in range(TILES):
                                last = nc.tensor.transpose(m_bank[1][:, t * P:(t + 1) * P], o[:, t, :], ident[:, :])
                            last.then_inc(oT2_done, 1)
                        if p == 6 and live(0):
                            if live(-1):
                                pe.wait_ge(oT_ready, (n - 1) * SHARES + 2)
                            weigh(n, r, 2)
                        if p == 6 and live(-2):
                            pe.wait_ge(yn_ready, (n - 2) + 1)
                            if live(3):
                                pe.wait_ge(v_ready, (n + 3) + 1)
                            elif live(-3):
                                pe.wait_ge(yT_ready, (n - 3) + 1)
                            for t in range(TILES):
                                last = nc.tensor.transpose(m_bank[0][:, t * P:(t + 1) * P], yn[r % 2][:, t, :], ident[:, :])
                            last.then_inc(yT_done, 1)
                        if p == 7 and live(-1):
                            pe.wait_ge(onT_ready, (n - 1) + 1)
                            for t in range(TILES):
                                last = nc.tensor.matmul(m_bank[1][:, t * P:(t + 1) * P], onT[:, t * P:(t + 1) * P], wo,
                                                        start=(t == 0), stop=(t == TILES - 1), skip_group_check=True)
                            last.then_inc(wo_done, 1)
                return step

            programs = {"sync": sync_program, "gpsimd": gpsimd_program, "vector": vector_program,
                        "scalar": scalar_program, "tensor": tensor_program}
            return programs, one_step, steps

        def run(attention_parts, first):
            programs, one_step, steps = attention_parts
            with nc.Block() as block:

                @block.sync
                def _(sp):
                    steps(sp, programs["sync"](sp), first)

                @block.gpsimd
                def _(pool):
                    steps(pool, programs["gpsimd"](pool), first)

                @block.vector
                def _(dve):
                    steps(dve, programs["vector"](dve), first)

                @block.scalar
                def _(act):
                    steps(act, programs["scalar"](act), first)

                @block.tensor
                def _(pe):
                    steps(pe, programs["tensor"](pe), first)

        def feed_forward(name, store, following=None):
            def s(what):
                return sem(f"{name}_{what}")

            pe_g, act_g, dve_g, index_in = s("pe_gate"), s("act_gate"), s("dve_gate"), s("index_in")
            wd_ready, wu_ready = [s(f"wd_ready{k}") for k in range(TOP)], [s(f"wu_ready{k}") for k in range(TOP)]
            down_done, h_ready, up_done, x_ready, stored = s("down_done"), s("h_ready"), s("up_done"), s("x_ready"), s("stored")
            AHEAD, BACK, LOOP0 = 2, 2, 6
            ROUNDS = (ITEMS - AHEAD - LOOP0) // RING
            STRETCHES = ((2, -5), (1, -4), (1, -3), (ROUNDS - 4, None)) if following else ((ROUNDS, None),)
            NBEST, WHICH, MIXED, HOT_T, BIASD, BIASU_PARTS = 3, 7, 14, 16, 17, 22

            def steps(engine, emit, ahead=None):
                def peeled(n):
                    emit(n, n % RING, lambda k: 0 <= n + k < ITEMS)
                for n in range(-AHEAD, LOOP0):
                    peeled(n)
                start = LOOP0
                for rounds, ahead_step in STRETCHES:
                    with engine.Fori(0, rounds) as i:
                        for u in range(RING):
                            emit(i * RING + (start + u), (start + u) % RING, lambda k: True)
                    start += rounds * RING
                    if ahead_step is not None:
                        ahead(ahead_step)
                for n in range(LOOP0 + ROUNDS * RING, ITEMS + BACK):
                    peeled(n)

            def experts_of_four(item, k, engine):
                at = bass.ds(item + k * ITEMS, RING)
                return nc.values_load_multi_w_load_instructions(index[0:1, at], engines=(engine.engine,),
                                                                min_val=0, max_val=EXPERTS - 1)[1]

            def second_weights(k, z):
                half = slice(HIDDEN * k, HIDDEN * (k + 1))
                return half, wu[z][half, :].unsqueeze(1)

            def ahead_steps(engine, kind):
                if not following:
                    return None
                programs, one_step, _ = following
                step = programs[kind](engine)
                return lambda n: one_step(step, n)

            with nc.Block() as block:

                @block.gpsimd
                def _(pool):
                    pool.wait_ge(index_in, 16 * TOP)
                    experts = [None]

                    def step(n, r, live):
                        if live(2):
                            z = (r + 2) % RING
                            if z == 0:
                                experts[0] = experts_of_four(n + 2, 0, pool)
                            if live(-2):
                                pool.wait_ge(down_done, (n - 2) + 1)
                            nc.gpsimd.tensor_copy(wd[z][:, 0:1, :], down_sb[:, bass.ds(experts[0][z], 1), :]).then_inc(wd_ready[0], 1)
                    steps(pool, step, ahead_steps(pool, "gpsimd"))

                @block.vector
                def _(dve):
                    count = [0]

                    def link(ins):
                        count[0] += 1
                        ins.then_inc(dve_g, 1)
                        dve.wait_ge(dve_g, count[0])

                    dve.wait_ge(pe_g, 1)
                    link(nc.vector.tensor_scalar(logit[:, :], banks[0][0:ITEMS, 0:EXPERTS], 1.0 / TOKENS, None, ALU.mult))
                    link(nc.vector.max(best[:, :], logit[:, :]))
                    link(nc.vector.tensor_scalar(nbest[:, :], best[:, 0:1], -1.0, None, ALU.mult))
                    dve.wait_ge(act_g, 1)
                    link(nc.vector.reciprocal(tsum[:, :], esum[:, :]))
                    link(nc.vector.tensor_scalar(gate[:, :], e[:, :], tsum[:, :], None, ALU.mult))
                    link(nc.vector.max(top[:, :], gate[:, :]))
                    link(nc.vector.max_index(which[:, :], top[:, :], gate[:, :]))
                    link(nc.vector.tensor_copy(whichf[:, :], which[:, 0:TOP]))
                    link(nc.vector.tensor_scalar(tsum[:, :], top[:, 0:1], top[:, 1:2], 1e-8, ALU.add, ALU.add))
                    link(nc.vector.reciprocal(tsum[:, :], tsum[:, :]))
                    link(nc.vector.tensor_scalar(wt[:, :], top[:, 0:TOP], tsum[:, :], None, ALU.mult))
                    for k in range(TOP):
                        nc.vector.tensor_copy(wide[:, k, :], wt[:, k:k + 1].broadcast_to([ITEMS, HIDDEN]))
                        last = nc.vector.tensor_scalar(hot[:, k, :], iota_sb[:, :], whichf[:, k:k + 1], None, ALU.is_equal)
                    link(last)
                    link(nc.vector.tensor_scalar(mix[:, :], hot[:, 0, :], wt[:, 0:1], None, ALU.mult))
                    link(nc.vector.scalar_tensor_tensor(out=mix[:, :], in0=hot[:, 1, :], scalar=wt[:, 1:2], in1=mix[:, :],
                                                        op0=ALU.mult, op1=ALU.add))
                    dve.wait_ge(pe_g, 2)
                    link(nc.vector.tensor_copy(weight[:, :], banks[1][:, 0:ITEMS]))
                    link(nc.vector.tensor_copy(hotT[:, :, :].rearrange("p a b -> p (a b)"), banks[2][0:EXPERTS, 0:(TOP + 3) * ITEMS]))
                    dve.wait_ge(pe_g, 3)
                    link(nc.vector.tensor_copy(biasd[:, :], banks[3][:, 0:ITEMS]))
                    link(nc.vector.tensor_copy(biasu[:, :], banks[4][0:3 * ITEMS, 0:WIDTH]))
                    link(nc.vector.tensor_copy(biasu_parts[:, :], biasu[:, :]))
                    link(nc.vector.tensor_tensor(biasu_rest[:, :], biasu[:, :], biasu_parts[:, :], ALU.subtract))
                    link(nc.vector.tensor_copy(biasu_mid[:, :], biasu_rest[:, :]))
                    mid_rows, lo_rows = slice(ITEMS, 2 * ITEMS), slice(2 * ITEMS, 3 * ITEMS)
                    nc.vector.tensor_copy(biasu_parts[mid_rows, :], biasu_mid[mid_rows, :])
                    link(nc.vector.tensor_tensor(biasu_parts[lo_rows, :], biasu_rest[lo_rows, :], biasu_mid[lo_rows, :], ALU.subtract))
                    assert count[0] == BIASU_PARTS

                    dve.wait_ge(index_in, 16 * TOP)
                    experts = [None]

                    def step(n, r, live):
                        if live(-2):
                            dve.wait_ge(up_done, (n - 2) + 1)
                            xs = x[:, bass.ds((n - 2) * TILES, TILES), :]
                            src = o_bank[r % 2][:, 0:TOKENS].rearrange("p (t d) -> p t d", t=TILES)
                            nc.vector.tensor_tensor(xs, xs, src, ALU.add).then_inc(x_ready, 1)
                        if live(2):
                            z = (r + 2) % RING
                            if z == 0:
                                experts[0] = experts_of_four(n + 2, 0, dve)
                            half, dst = second_weights(0, z)
                            nc.vector.tensor_scalar(dst, up_sb[half, bass.ds(experts[0][z], 1), :],
                                                    weight[half, bass.ds(n + 2, 1)], None, ALU.mult).then_inc(wu_ready[0], 1)
                    following_step = ahead_steps(dve, "vector")

                    def ahead(n):
                        wait_apart(dve, x_ready, (n + 5) + 1)
                        following_step(n)
                    steps(dve, step, ahead)

                @block.scalar
                def _(act):
                    act.wait_ge(dve_g, NBEST)
                    nc.scalar.activation(e[:, :], logit[:, :], ACT.Exp, bias=nbest[:, :], accum_out=esum[:, :]).then_inc(act_g, 1)
                    nc.scalar.preload_act_table(ACT.Gelu)
                    act.wait_ge(dve_g, BIASD)
                    act.wait_ge(index_in, 16 * TOP)
                    experts = [None]

                    def step(n, r, live):
                        if live(0):
                            act.wait_ge(down_done, n + 1)
                            if live(-2):
                                act.wait_ge(up_done, (n - 2) + 1)
                            nc.scalar.activation(hT[r % 2][:, :], t_bank[r % 2][:, 0:TOKENS], ACT.Gelu,
                                                 bias=biasd[:, bass.ds(n, 1)]).then_inc(h_ready, 1)
                        if live(2):
                            z = (r + 2) % RING
                            if z == 0:
                                experts[0] = experts_of_four(n + 2, 1, act)
                            nc.scalar.copy(wd[z][:, 1:2, :], down_sb[:, bass.ds(experts[0][z], 1), :]).then_inc(wd_ready[1], 1)
                            half, dst = second_weights(1, z)
                            nc.scalar.activation(dst, up_sb[half, bass.ds(experts[0][z], 1), :], ACT.Copy,
                                                 scale=weight[half, bass.ds(n + 2, 1)]).then_inc(wu_ready[1], 1)
                    steps(act, step, ahead_steps(act, "scalar"))

                @block.tensor
                def _(pe):
                    nc.tensor.matmul(banks[0][0:ITEMS, 0:EXPERTS], pooled[:, :], gate_sb[:, :], start=True, stop=True).then_inc(pe_g, 1)
                    pe.wait_ge(dve_g, MIXED)
                    nc.tensor.transpose(banks[1][:, 0:ITEMS], wide[:, :, :].rearrange("p a b -> p (a b)"), ident[0:ITEMS, 0:ITEMS])
                    for k in range(TOP + 3):
                        src = hot[:, k, :] if k < TOP else mix[:, :]
                        last = nc.tensor.transpose(banks[2][0:EXPERTS, k * ITEMS:(k + 1) * ITEMS], src, ident[0:ITEMS, 0:ITEMS])
                    last.then_inc(pe_g, 1)
                    pe.wait_ge(dve_g, HOT_T)
                    for k in range(TOP):
                        nc.tensor.matmul(banks[3][HIDDEN * k:HIDDEN * (k + 1), 0:ITEMS], downb_sb[:, :], hotT[:, k, :], start=True, stop=True)
                    nc.tensor.matmul(banks[4][0:3 * ITEMS, 0:WIDTH], hotT[:, TOP:, :].rearrange("p a b -> p (a b)"), upb_sb[:, :],
                                     start=True, stop=True).then_inc(pe_g, 1)
                    pe.wait_ge(dve_g, BIASU_PARTS)

                    def step(n, r, live):
                        if live(0):
                            for k in range(TOP):
                                pe.wait_ge(wd_ready[k], n + 1)
                            if live(-2):
                                pe.wait_ge(h_ready, (n - 2) + 1)
                            nc.tensor.matmul(t_bank[r % 2][:, 0:TOKENS], wd[r][:, :, :].rearrange("p a b -> p (a b)"),
                                             normT[:, bass.ds(n, 1), :], start=True, stop=True).then_inc(down_done, 1)
                        if live(-2):
                            z = (r - 2) % RING
                            if live(-4):
                                pe.wait_ge(x_ready, (n - 4) + 1)
                            acc = o_bank[r % 2]
                            nc.tensor.matmul(acc[:, 0:TOKENS].rearrange("p (t d) -> p t d", t=TILES),
                                             pick[:, bass.ds(n - 2, 1)].broadcast_to([3 * ITEMS, P]),
                                             biasu_parts[:, :].unsqueeze(1).broadcast_to([3 * ITEMS, TILES, WIDTH]),
                                             start=True, stop=False, skip_group_check=True)
                            for k in range(TOP):
                                pe.wait_ge(wu_ready[k], (n - 2) + 1)
                            pe.wait_ge(h_ready, (n - 2) + 1)
                            for t in range(TILES):
                                last = nc.tensor.matmul(acc[:, t * P:(t + 1) * P], hT[r % 2][:, t * P:(t + 1) * P], wu[z][:, :],
                                                        start=False, stop=(t == TILES - 1), skip_group_check=True)
                            last.then_inc(up_done, 1)
                    steps(pe, step, ahead_steps(pe, "tensor"))

                @block.sync
                def _(sp):
                    sp.wait_ge(dve_g, WHICH)
                    for k in range(TOP):
                        sp.dma_start(index[0:1, k * ITEMS:(k + 1) * ITEMS], which[:, k:k + 1]).then_inc(index_in, 16)
                    sp.wait_ge(index_in, 16 * TOP)
                    if not store:
                        constant_rows(sp, 1)
                        following_step = ahead_steps(sp, "sync")
                        for n in (-5, -4, -3):
                            following_step(n)
                    if store:
                        def step(n, r, live):
                            if live(-2):
                                sp.wait_ge(x_ready, (n - 2) + 1)
                                at = bass.ds((n - 2) * TILES, TILES)
                                sp.dma_start(out_dram[:, at, :], x[:, at, :]).then_inc(stored, 16)
                        steps(sp, step)
                        sp.wait_ge(stored, 16 * ITEMS)

        phase_a = attention("a", wa, True, float(HEAD) ** -0.5, True)
        phase_b = attention("b", wb, False, float(WIDTH) ** -0.5, False)
        run(phase_a, -5)
        feed_forward("fa", False, phase_b)
        run(phase_b, -2)
        feed_forward("fb", True)


def kernel(L0_attn_a_x, L0_attn_a_Wq, L0_attn_a_bq, L0_attn_a_Wk, L0_attn_a_bk, L0_attn_a_Wv, L0_attn_a_bv, L0_attn_a_Wo,
           L0_attn_b_w_qkv, L0_attn_b_w_out, L0_ffn_gate_w, L0_ffn_down_w, L0_ffn_down_b, L0_ffn_up_w, L0_ffn_up_b):
    import ml_dtypes
    import concourse.bacc as bacc
    from concourse.bass_utils import run_bass_kernel_spmd

    def heads_last(m):
        m = np.asarray(m)
        return m.reshape(m.shape[0], PAIRS, 2, HEAD).transpose(0, 2, 3, 1).reshape(m.shape[0], WIDTH)

    def shared(m):
        m = np.asarray(m)
        return m.reshape(SHARES, IN_SHARE, PER_GROUP, HEAD, -1).transpose(0, 2, 1, 3, 4).reshape(m.shape)

    t = lambda m: np.asarray(m).T
    col = lambda v: np.asarray(v).reshape(1, WIDTH)
    w_qkv = np.asarray(L0_attn_b_w_qkv)
    arrays = {
        "x": np.asarray(L0_attn_a_x),
        "attn_a": np.concatenate([heads_last(t(L0_attn_a_Wq)), heads_last(t(L0_attn_a_Wk)), t(L0_attn_a_Wv), shared(t(L0_attn_a_Wo)),
                                  heads_last(col(L0_attn_a_bq)).T, heads_last(col(L0_attn_a_bk)).T, shared(col(L0_attn_a_bv).T)], 1),
        "attn_b": np.concatenate([heads_last(w_qkv[:, 0:128]), heads_last(w_qkv[:, 128:256]), w_qkv[:, 256:384],
                                  shared(L0_attn_b_w_out)], 1),
        "gate_w": t(L0_ffn_gate_w),
        "down_w": np.asarray(L0_ffn_down_w).transpose(2, 0, 1),
        "down_b": np.asarray(L0_ffn_down_b),
        "up_w": np.asarray(L0_ffn_up_w).transpose(2, 0, 1),
        "up_b": np.asarray(L0_ffn_up_b),
        "tail": rows_of_constants().astype(ml_dtypes.bfloat16),
        "ident": np.eye(P, dtype=np.float32),
        "iota": np.tile(np.arange(EXPERTS, dtype=np.float32), (ITEMS, 1)),
        "pick": np.tile(np.eye(ITEMS), (3, 1)).astype(ml_dtypes.bfloat16),
    }
    arrays = {f"in_{k}": np.ascontiguousarray(v) for k, v in arrays.items()}
    nc = bacc.Bacc("TRN2", target_bir_lowering=False, num_devices=1)
    args = [nc.dram_tensor(k, v.shape, mybir.dt.from_np(v.dtype), kind="ExternalInput").ap() for k, v in arrays.items()]
    out = nc.dram_tensor("out", (ITEMS, TOKENS, WIDTH), FP32, kind="ExternalOutput").ap()
    build(nc, *args, out)
    r = run_bass_kernel_spmd(nc, [arrays], core_ids=[0])
    return r.results[0]["out"]
```
